# Optimizing a Trainium2 kernel written in Bass

```python
import numpy as np
import jax
import jax.numpy as jnp

def _softmax(x, axis=-1):
    return jax.nn.softmax(x, axis=axis)

def _gelu(x):
    return jax.nn.gelu(x, approximate=True)

def _silu(x):
    return jax.nn.silu(x)

def _sigmoid(x):
    return jax.nn.sigmoid(x)

def _layernorm(x, axis=-1, eps=1e-05):
    m = jnp.mean(x, axis=axis, keepdims=True)
    v = jnp.var(x, axis=axis, keepdims=True)
    return (x - m) / jnp.sqrt(v + eps)

def _scatter_add(tgt, idx, src, axis=0):
    return tgt.at[idx].add(src)

def _segment_sum(src, seg, n):
    return jax.ops.segment_sum(src, seg, n)
kernel_name = 'mk_macaron_d1_jaxref_r8_6f883d'

def setup_inputs(seed: int=0):
    np.random.seed(seed)
    _w = jnp.asarray

    def _L0_attn_setup():
        import jax, jax.numpy as jnp
        import numpy as np
        from math import sqrt
        N_HEAD = 16
        W_SCALE = 0.02

        def _reference_tuple_inner(x, W_dq, W_uq, W_dkv, W_uk, W_uv, W_o):
            B, T, C = x.shape
            nh = N_HEAD
            hs = C // nh
            n_kvl = W_dkv.shape[0]
            k_eff = (W_dq.T @ W_uq.T @ W_uk).reshape(nh, hs, n_kvl)
            v_eff = jnp.transpose((W_uv.T @ W_o.T).reshape(n_kvl, nh, hs), (1, 0, 2))
            c_kv = x @ W_dkv.T
            q = x @ W_dq.T @ W_uq.T
            q = q.reshape(B, T, nh, hs)
            q_lat = jnp.einsum('bqhd,hdl->bhql', q, k_eff)
            attn = jnp.einsum('bhql,bkl->bhqk', q_lat, c_kv) / sqrt(hs)
            causal = jnp.tril(jnp.ones((T, T), dtype=bool))
            attn = jnp.where(causal[None, None], attn, -jnp.inf)
            attn = jax.nn.softmax(attn, axis=-1)
            y_lat = jnp.einsum('bhqk,bkl->bhql', attn, c_kv)
            y = jnp.einsum('bhql,hld->bqhd', y_lat, v_eff).reshape(B, T, C)
            return (y, c_kv)
        key = jax.random.key(seed)
        ks = jax.random.split(key, 7)
        B, T, C = (2, 256, 128)
        QL, KVL = (64, 64)
        return {'x': jax.random.normal(ks[0], (B, T, C), dtype=jnp.float32), 'W_dq': jax.random.normal(ks[1], (QL, C), dtype=jnp.float32) * W_SCALE, 'W_uq': jax.random.normal(ks[2], (C, QL), dtype=jnp.float32) * W_SCALE, 'W_dkv': jax.random.normal(ks[3], (KVL, C), dtype=jnp.float32) * W_SCALE, 'W_uk': jax.random.normal(ks[4], (C, KVL), dtype=jnp.float32) * W_SCALE, 'W_uv': jax.random.normal(ks[5], (C, KVL), dtype=jnp.float32) * W_SCALE, 'W_o': jax.random.normal(ks[6], (C, C), dtype=jnp.float32) * W_SCALE}
    _L0_attn_in = _L0_attn_setup()

    def _L0_ffn_setup():
        import jax, jax.numpy as jnp
        import numpy as np
        DIM = 128
        DEPTH = 2
        HEADS = 8
        DIM_HEAD = 64
        WINDOW = 64
        INNER = HEADS * DIM_HEAD
        HID = int(DIM * 4 * 2 / 3)
        B, N = (2, 1024)
        QK_SCALE = 8.0

        def shift_token(t):
            t1, t2 = jnp.split(t, 2, axis=-1)
            t2 = jnp.pad(t2, ((0, 0), (1, 0), (0, 0)))[:, :-1]
            return jnp.concatenate([t1, t2], axis=-1)

        def l2norm(t):
            return t / jnp.clip(jnp.linalg.norm(t, axis=-1, keepdims=True), 1e-12)

        def rotate_half(x):
            x1, x2 = jnp.split(x, 2, axis=-1)
            return jnp.concatenate([-x2, x1], axis=-1)

        def rotary_xpos(q, k):
            n = q.shape[-2]
            half_idx = jnp.arange(0, DIM_HEAD, 2, dtype=jnp.float32)
            inv_freq = 1.0 / 10000.0 ** (half_idx / DIM_HEAD)
            t = jnp.arange(n, dtype=jnp.float32)
            freqs = t[:, None] * inv_freq[None, :]
            freqs = jnp.concatenate([freqs, freqs], axis=-1)
            base = (half_idx + 0.4 * DIM_HEAD) / (1.4 * DIM_HEAD)
            power = (t - n // 2) / float(WINDOW // 2)
            scale = base[None, :] ** power[:, None]
            scale = jnp.concatenate([scale, scale], axis=-1)
            cos, sin = (jnp.cos(freqs), jnp.sin(freqs))
            q = q * cos * scale + rotate_half(q) * sin * scale
            k = k * cos / scale + rotate_half(k) * sin / scale
            return (q, k)

        def local_attention(q, k, v):
            b, h, n, d = q.shape
            w = n // WINDOW
            bq = q.reshape(b, h, w, WINDOW, d) * QK_SCALE
            bk = k.reshape(b, h, w, WINDOW, d)
            bv = v.reshape(b, h, w, WINDOW, d)

            def look_around(t):
                p = jnp.pad(t, ((0, 0), (0, 0), (1, 0), (0, 0), (0, 0)))
                return jnp.concatenate([p[:, :, :w], p[:, :, 1:]], axis=3)
            bk, bv = (look_around(bk), look_around(bv))
            bt = jnp.arange(n).reshape(w, WINDOW)
            btp = jnp.pad(bt, ((1, 0), (0, 0)), constant_values=-1)
            btk = jnp.concatenate([btp[:w], btp[1:]], axis=1)
            sim = jnp.einsum('bhwid,bhwjd->bhwij', bq, bk)
            i = bt[:, :, None]
            j = btk[:, None, :]
            mask = (i < j) | (i > j + WINDOW) | (j == -1)
            sim = jnp.where(mask, -jnp.finfo(sim.dtype).max, sim)
            attn = jax.nn.softmax(sim, axis=-1)
            out = jnp.einsum('bhwij,bhwjd->bhwid', attn, bv)
            return out.reshape(b, h, n, d)

        def _layer(x, wqkv, qs, ksc, wo, lg, lb, w1, b1, w2, b2):
            b, n, _ = x.shape
            h = shift_token(x)
            qkv = h @ wqkv
            q, k, v = jnp.split(qkv, 3, axis=-1)
            to_heads = lambda t: t.reshape(b, n, HEADS, DIM_HEAD).transpose(0, 2, 1, 3)
            q, k, v = (to_heads(q), to_heads(k), to_heads(v))
            q = l2norm(q) * qs
            k = l2norm(k) * ksc
            q, k = rotary_xpos(q, k)
            o = local_attention(q, k, v)
            o = o.transpose(0, 2, 1, 3).reshape(b, n, INNER)
            x = x + o @ wo
            h = shift_token(x)
            mu = h.mean(-1, keepdims=True)
            var = h.var(-1, keepdims=True)
            h = (h - mu) / jnp.sqrt(var + 1e-05) * lg + lb
            h = h @ w1 + b1
            a, g = jnp.split(h, 2, axis=-1)
            h = a * jax.nn.gelu(g, approximate=False)
            x = x + h @ w2 + b2
            return x
        key = jax.random.key(seed)
        ks = jax.random.split(key, 6)
        return {'x': jax.random.normal(ks[0], (B, N, DIM), jnp.float32), 'wqkv': jax.random.normal(ks[1], (DEPTH, DIM, 3 * INNER), jnp.float32) * 0.02, 'q_scale': jnp.ones((DEPTH, DIM_HEAD), jnp.float32), 'k_scale': jnp.ones((DEPTH, DIM_HEAD), jnp.float32), 'wo': jax.random.normal(ks[2], (DEPTH, INNER, DIM), jnp.float32) * 0.02, 'ln_g': jnp.ones((DEPTH, DIM), jnp.float32), 'ln_b': jnp.zeros((DEPTH, DIM), jnp.float32), 'w1': jax.random.normal(ks[3], (DEPTH, DIM, 2 * HID), jnp.float32) * 0.02, 'b1': jnp.zeros((DEPTH, 2 * HID), jnp.float32), 'w2': jax.random.normal(ks[4], (DEPTH, HID, DIM), jnp.float32) * 0.02, 'b2': jnp.zeros((DEPTH, DIM), jnp.float32)}
    _L0_ffn_in = _L0_ffn_setup()
    _d = {'L0_attn_x': _L0_attn_in['x'], 'L0_attn_W_dq': _L0_attn_in['W_dq'], 'L0_attn_W_uq': _L0_attn_in['W_uq'], 'L0_attn_W_dkv': _L0_attn_in['W_dkv'], 'L0_attn_W_uk': _L0_attn_in['W_uk'], 'L0_attn_W_uv': _L0_attn_in['W_uv'], 'L0_attn_W_o': _L0_attn_in['W_o'], 'L0_ffn_wqkv': _L0_ffn_in['wqkv'], 'L0_ffn_q_scale': _L0_ffn_in['q_scale'], 'L0_ffn_k_scale': _L0_ffn_in['k_scale'], 'L0_ffn_wo': _L0_ffn_in['wo'], 'L0_ffn_ln_g': _L0_ffn_in['ln_g'], 'L0_ffn_ln_b': _L0_ffn_in['ln_b'], 'L0_ffn_w1': _L0_ffn_in['w1'], 'L0_ffn_b1': _L0_ffn_in['b1'], 'L0_ffn_w2': _L0_ffn_in['w2'], 'L0_ffn_b2': _L0_ffn_in['b2']}
    _x0 = _d['L0_attn_x']
    _d['L0_attn_x'] = jax.random.normal(jax.random.fold_in(jax.random.key(seed), 1), (8, 512, 128), dtype=_x0.dtype)
    del _x0
    return _d

def reference(L0_attn_x, L0_attn_W_dq, L0_attn_W_uq, L0_attn_W_dkv, L0_attn_W_uk, L0_attn_W_uv, L0_attn_W_o, L0_ffn_wqkv, L0_ffn_q_scale, L0_ffn_k_scale, L0_ffn_wo, L0_ffn_ln_g, L0_ffn_ln_b, L0_ffn_w1, L0_ffn_b1, L0_ffn_w2, L0_ffn_b2):

    def _L0_attn_ref(x, W_dq, W_uq, W_dkv, W_uk, W_uv, W_o):
        import jax, jax.numpy as jnp
        import numpy as np
        from math import sqrt
        N_HEAD = 16
        W_SCALE = 0.02

        def _reference_tuple_inner(x, W_dq, W_uq, W_dkv, W_uk, W_uv, W_o):
            B, T, C = x.shape
            nh = N_HEAD
            hs = C // nh
            n_kvl = W_dkv.shape[0]
            k_eff = (W_dq.T @ W_uq.T @ W_uk).reshape(nh, hs, n_kvl)
            v_eff = jnp.transpose((W_uv.T @ W_o.T).reshape(n_kvl, nh, hs), (1, 0, 2))
            c_kv = x @ W_dkv.T
            q = x @ W_dq.T @ W_uq.T
            q = q.reshape(B, T, nh, hs)
            q_lat = jnp.einsum('bqhd,hdl->bhql', q, k_eff)
            attn = jnp.einsum('bhql,bkl->bhqk', q_lat, c_kv) / sqrt(hs)
            causal = jnp.tril(jnp.ones((T, T), dtype=bool))
            attn = jnp.where(causal[None, None], attn, -jnp.inf)
            attn = jax.nn.softmax(attn, axis=-1)
            y_lat = jnp.einsum('bhqk,bkl->bhql', attn, c_kv)
            y = jnp.einsum('bhql,hld->bqhd', y_lat, v_eff).reshape(B, T, C)
            return (y, c_kv)
        return _reference_tuple_inner(x, W_dq, W_uq, W_dkv, W_uk, W_uv, W_o)[0]

    def _L0_ffn_ref(x, wqkv, q_scale, k_scale, wo, ln_g, ln_b, w1, b1, w2, b2):
        import jax, jax.numpy as jnp
        import numpy as np
        DIM = 128
        DEPTH = 2
        HEADS = 8
        DIM_HEAD = 64
        WINDOW = 64
        INNER = HEADS * DIM_HEAD
        HID = int(DIM * 4 * 2 / 3)
        B, N = (2, 1024)
        QK_SCALE = 8.0

        def shift_token(t):
            t1, t2 = jnp.split(t, 2, axis=-1)
            t2 = jnp.pad(t2, ((0, 0), (1, 0), (0, 0)))[:, :-1]
            return jnp.concatenate([t1, t2], axis=-1)

        def l2norm(t):
            return t / jnp.clip(jnp.linalg.norm(t, axis=-1, keepdims=True), 1e-12)

        def rotate_half(x):
            x1, x2 = jnp.split(x, 2, axis=-1)
            return jnp.concatenate([-x2, x1], axis=-1)

        def rotary_xpos(q, k):
            n = q.shape[-2]
            half_idx = jnp.arange(0, DIM_HEAD, 2, dtype=jnp.float32)
            inv_freq = 1.0 / 10000.0 ** (half_idx / DIM_HEAD)
            t = jnp.arange(n, dtype=jnp.float32)
            freqs = t[:, None] * inv_freq[None, :]
            freqs = jnp.concatenate([freqs, freqs], axis=-1)
            base = (half_idx + 0.4 * DIM_HEAD) / (1.4 * DIM_HEAD)
            power = (t - n // 2) / float(WINDOW // 2)
            scale = base[None, :] ** power[:, None]
            scale = jnp.concatenate([scale, scale], axis=-1)
            cos, sin = (jnp.cos(freqs), jnp.sin(freqs))
            q = q * cos * scale + rotate_half(q) * sin * scale
            k = k * cos / scale + rotate_half(k) * sin / scale
            return (q, k)

        def local_attention(q, k, v):
            b, h, n, d = q.shape
            w = n // WINDOW
            bq = q.reshape(b, h, w, WINDOW, d) * QK_SCALE
            bk = k.reshape(b, h, w, WINDOW, d)
            bv = v.reshape(b, h, w, WINDOW, d)

            def look_around(t):
                p = jnp.pad(t, ((0, 0), (0, 0), (1, 0), (0, 0), (0, 0)))
                return jnp.concatenate([p[:, :, :w], p[:, :, 1:]], axis=3)
            bk, bv = (look_around(bk), look_around(bv))
            bt = jnp.arange(n).reshape(w, WINDOW)
            btp = jnp.pad(bt, ((1, 0), (0, 0)), constant_values=-1)
            btk = jnp.concatenate([btp[:w], btp[1:]], axis=1)
            sim = jnp.einsum('bhwid,bhwjd->bhwij', bq, bk)
            i = bt[:, :, None]
            j = btk[:, None, :]
            mask = (i < j) | (i > j + WINDOW) | (j == -1)
            sim = jnp.where(mask, -jnp.finfo(sim.dtype).max, sim)
            attn = jax.nn.softmax(sim, axis=-1)
            out = jnp.einsum('bhwij,bhwjd->bhwid', attn, bv)
            return out.reshape(b, h, n, d)

        def _layer(x, wqkv, qs, ksc, wo, lg, lb, w1, b1, w2, b2):
            b, n, _ = x.shape
            h = shift_token(x)
            qkv = h @ wqkv
            q, k, v = jnp.split(qkv, 3, axis=-1)
            to_heads = lambda t: t.reshape(b, n, HEADS, DIM_HEAD).transpose(0, 2, 1, 3)
            q, k, v = (to_heads(q), to_heads(k), to_heads(v))
            q = l2norm(q) * qs
            k = l2norm(k) * ksc
            q, k = rotary_xpos(q, k)
            o = local_attention(q, k, v)
            o = o.transpose(0, 2, 1, 3).reshape(b, n, INNER)
            x = x + o @ wo
            h = shift_token(x)
            mu = h.mean(-1, keepdims=True)
            var = h.var(-1, keepdims=True)
            h = (h - mu) / jnp.sqrt(var + 1e-05) * lg + lb
            h = h @ w1 + b1
            a, g = jnp.split(h, 2, axis=-1)
            h = a * jax.nn.gelu(g, approximate=False)
            x = x + h @ w2 + b2
            return x
        for l in range(DEPTH):
            x = _layer(x, wqkv[l], q_scale[l], k_scale[l], wo[l], ln_g[l], ln_b[l], w1[l], b1[l], w2[l], b2[l])
        return x
    x = L0_attn_x
    x = x + 0.5 * _L0_ffn_ref(_layernorm(x, axis=-1), L0_ffn_wqkv, L0_ffn_q_scale, L0_ffn_k_scale, L0_ffn_wo, L0_ffn_ln_g, L0_ffn_ln_b, L0_ffn_w1, L0_ffn_b1, L0_ffn_w2, L0_ffn_b2)
    x = x + _L0_attn_ref(_layernorm(x, axis=-1), L0_attn_W_dq, L0_attn_W_uq, L0_attn_W_dkv, L0_attn_W_uk, L0_attn_W_uv, L0_attn_W_o)
    x = x + 0.5 * _L0_ffn_ref(_layernorm(x, axis=-1), L0_ffn_wqkv, L0_ffn_q_scale, L0_ffn_k_scale, L0_ffn_wo, L0_ffn_ln_g, L0_ffn_ln_b, L0_ffn_w1, L0_ffn_b1, L0_ffn_w2, L0_ffn_b2)
    return x

_drawn_inputs = setup_inputs


def setup_inputs(seed=0):
    import zlib

    import numpy as np

    out = dict(_drawn_inputs(seed))
    spreads = {'L0_ffn_q_scale': (1.0, 0.6),
     'L0_ffn_k_scale': (1.0, 0.6),
     'L0_ffn_ln_g': (1.0, 0.6),
     'L0_ffn_ln_b': (0.0, 0.8),
     'L0_ffn_b1': (0.0, 0.8),
     'L0_ffn_b2': (0.0, 0.1)}
    factors = {'L0_attn_W_dq': 8.0,
     'L0_attn_W_uq': 8.0,
     'L0_attn_W_dkv': 8.0,
     'L0_attn_W_uk': 8.0,
     'L0_attn_W_uv': 8.0,
     'L0_attn_W_o': 8.0,
     'L0_ffn_wqkv': 3.166,
     'L0_ffn_wo': 3.154,
     'L0_ffn_w1': 5.291,
     'L0_ffn_w2': 5.211}
    for name, (base, spread) in spreads.items():
        noise = np.random.default_rng([zlib.crc32(name.encode()), seed]).standard_normal(out[name].shape)
        drawn = base * np.exp(spread * noise) if base else spread * noise
        out[name] = jnp.asarray(drawn.astype(out[name].dtype))
    for name, factor in factors.items():
        out[name] = (out[name] * factor).astype(out[name].dtype)
    return out
```

```python
from contextlib import ExitStack

import numpy as np
import concourse.bass as bass
from concourse import mybir

F32 = mybir.dt.float32
BF16 = mybir.dt.bfloat16
ALU = mybir.AluOpType
ACT = mybir.ActivationFunctionType
AX_X = mybir.AxisListType.X

P = 128
W = 64
NH, DH = 8, 64
NG, DG = 16, 8
EPS = 1e-5
BIG = -1e30
LG = 4


def shape_constants(T):
    half = np.arange(0, DH, 2, dtype=np.float32)
    inv = (1.0 / np.float32(10000.0) ** (half / np.float32(DH))).astype(np.float32)
    t = np.arange(T, dtype=np.float32)
    f = t[:, None] * inv[None, :]
    base = ((half + np.float32(0.4 * DH)) / np.float32(1.4 * DH)).astype(np.float32)
    power = ((t - T // 2) / np.float32(W // 2)).astype(np.float32)
    s = (base[None, :] ** power[:, None]).astype(np.float32)
    c, sn = np.cos(f), np.sin(f)
    tab = np.stack([np.concatenate([c * s, c * s], -1), np.concatenate([-sn * s, sn * s], -1),
                    np.concatenate([c / s, c / s], -1), np.concatenate([-sn / s, sn / s], -1)], 1)
    rope = tab.reshape(T // P, P, 4, DH).transpose(1, 0, 2, 3).reshape(P, -1).astype(np.float32)
    q, k = np.arange(P)[:, None] % W, np.arange(P)[None, :]
    band = np.where((k <= W + q) & (k >= q), 0.0, BIG).astype(np.float32)
    first = band.copy()
    first[:W, :W] = BIG
    causal = np.where(np.arange(P)[None, :] <= np.arange(P)[:, None], 0.0, BIG).astype(np.float32)
    headsel = (np.arange(P)[:, None] // DG == np.arange(NG)[None, :]).astype(np.float32)
    return np.concatenate([rope, band, first, causal, np.eye(P, dtype=np.float32), headsel], 1)


def macaron(nc, x, W_dq, W_uq, W_dkv, W_uk, W_uv, W_o, wqkv, q_scale, k_scale, wo, ln_g, ln_b,
            w1, b1, w2, b2, consts, out):
    B, T, C = x.shape
    DEPTH, HID = w2.shape[0], w2.shape[1]
    NT = T // P
    NB = 2
    NS = NB * NT
    QL = W_dq.shape[0]
    HC = -(-HID // 3)
    HCS = [HC, HC, HID - 2 * HC]
    CH = NH * DH // P
    top = ExitStack()
    with top:
        stack = [top]
        phase = [0]

        def sb(name, shape, dt=F32):
            return stack[-1].enter_context(nc.sbuf_tensor(f"{name}_{phase[0]}", shape, dt))

        def sem(name):
            return stack[-1].enter_context(nc.semaphore(f"{name}_{phase[0]}"))

        BK = [top.enter_context(nc.psum_tensor(f"bank{i}", [P, 512], F32)) for i in range(8)]

        ROPE = NT * 4 * DH
        cst = sb("cst", [P, ROPE + 4 * P + NG])
        ident = cst[:, ROPE + 3 * P:ROPE + 4 * P]
        headsel = cst[:, ROPE + 4 * P:ROPE + 4 * P + NG]
        maskb = sb("maskb", [P, 3, P], BF16)
        identb = sb("identb", [P, P], BF16)
        ropet = sb("ropet", [P, DEPTH, NT, 4, DH])
        wqkv_s = sb("wqkv_s", [P, DEPTH, 3 * NH * DH])
        wo_s = sb("wo_s", [P, DEPTH, CH, P])
        w1_s = sb("w1_s", [P, DEPTH, 2 * HID])
        w2_s = sb("w2_s", [HC, DEPTH, 3, P])
        b1_s = sb("b1_s", [HC, DEPTH, 2, 3])
        b2_s = sb("b2_s", [P, DEPTH, P])
        lng = sb("lng", [P, DEPTH])
        lnb = sb("lnb", [P, DEPTH])
        meanw = sb("meanw", [P, P])
        ones = sb("ones", [P, P])
        mhalf = sb("mhalf", [P, 2 * NH])
        Wq_s = sb("Wq_s", [P, P])
        Wk_s = sb("Wk_s", [P, P])
        Wv_s = sb("Wv_s", [P, P])
        X = sb("X", [P, NS, P])
        U = sb("U", [P, NS, P])
        stats = sb("stats", [P, NS, 6])
        mv = sb("mv", [P, NS, 2])
        rstd = sb("rstd", [P, NS])

        def end_phase(sems):
            for s in sems:
                nc.sync.sem_clear(s)
            nc.all_engine_barrier()
            phase[0] += 1

        with ExitStack() as scope:
            stack.append(scope)
            qs = sb("qs", [P, DEPTH, 2, DH])
            ks = sb("ks", [P, DEPTH, DH])
            dq = sb("dq", [QL, P]); uq = sb("uq", [P, QL]); dkv = sb("dkv", [QL, P])
            uk = sb("uk", [P, QL]); uv = sb("uv", [P, QL]); wom = sb("wom", [P, P])
            uqT = sb("uqT", [QL, P]); woT = sb("woT", [P, P]); WqT = sb("WqT", [P, P])
            keT = sb("keT", [QL, P]); ve = sb("ve", [QL, P])
            b1raw = sb("b1raw", [HC, DEPTH, 2, 3])
            loaded = sem("loaded"); preset = sem("preset"); mm = sem("mm"); copied = sem("copied")
            LOADS = [0]
            with nc.Block() as block:
                @block.sync
                def _(sp):
                    def load(dst, src):
                        sp.dma_start(dst, src).then_inc(loaded, 16)
                        LOADS[0] += 16
                    load(cst[:, :], consts)
                    load(dq[:, :], W_dq); load(uq[:, :], W_uq); load(dkv[:, :], W_dkv)
                    load(uk[:, :], W_uk); load(uv[:, :], W_uv); load(wom[:, :], W_o)
                    for l in range(DEPTH):
                        load(wqkv_s[:, l, :], wqkv[l])
                        load(wo_s[:, l, :, :], wo[l].rearrange("(c p) n -> p c n", p=P))
                        load(w1_s[:, l, :], w1[l])
                        for c in range(3):
                            load(w2_s[0:HCS[c], l, c, :], w2[l][c * HC:c * HC + HCS[c], :])
                            for e in range(2):
                                o = e * HID + c * HC
                                load(b1raw[0:HCS[c], l, e, c:c + 1],
                                     b1[l][o:o + HCS[c]].rearrange("(p a) -> p a", a=1))
                        load(b2_s[:, l, :], b2[l:l + 1, :].broadcast_to([P, P]))
                        load(qs[:, l, 0, :], q_scale[l:l + 1, :].broadcast_to([P, DH]))
                        load(qs[:, l, 1, :], k_scale[l:l + 1, :].broadcast_to([P, DH]))
                        load(lng[:, l:l + 1], ln_g[l].rearrange("(p a) -> p a", a=1))
                        load(lnb[:, l:l + 1], ln_b[l].rearrange("(p a) -> p a", a=1))
                NL = LOADS[0]

                @block.gpsimd
                def _(pool):
                    nc.gpsimd.memset(meanw[:, :], 1.0 / C).then_inc(preset, 1)
                    nc.gpsimd.memset(ones[:, :], 1.0).then_inc(preset, 1)
                    nc.gpsimd.memset(mhalf[:, :], -0.5).then_inc(preset, 1)

                @block.tensor
                def _(pe):
                    pe.wait_ge(loaded, NL)
                    pe.transpose(BK[0][0:QL, 0:P], uq[:, :], ident).then_inc(mm, 1)
                    pe.transpose(BK[1][:, 0:P], wom[:, :], ident).then_inc(mm, 1)
                    for l in range(DEPTH):
                        for e in range(2):
                            for c in range(3):
                                o = e * HID + c * HC
                                j = (l * 2 + e) * 3 + c
                                last = nc.tensor.matmul(BK[2][0:HCS[c], j:j + 1], w1_s[:, l, o:o + HCS[c]],
                                                        lnb[:, l:l + 1], start=True, stop=True)
                    last.then_inc(mm, 1)
                    pe.wait_ge(copied, 1)
                    nc.tensor.matmul(BK[3][:, 0:P], uqT[:, :], dq[:, :], start=True, stop=True).then_inc(mm, 1)
                    nc.tensor.matmul(BK[4][:, 0:P], dq[:, :], uqT[:, :], start=True, stop=True).then_inc(mm, 1)
                    pe.wait_ge(copied, 2)
                    nc.tensor.matmul(BK[5][0:QL, 0:P], uv[:, :], woT[:, :], start=True, stop=True).then_inc(mm, 1)
                    pe.wait_ge(copied, 3)
                    nc.tensor.matmul(BK[6][0:QL, 0:P], uk[:, :], WqT[:, :], start=True, stop=True).then_inc(mm, 1)
                    pe.wait_ge(copied, 5)
                    nc.tensor.matmul(BK[0][:, 0:P], dkv[:, :], ve[:, :], start=True, stop=True).then_inc(mm, 1)
                    pe.wait_ge(copied, 6)
                    nc.tensor.matmul(BK[1][:, 0:P], dkv[:, :], keT[:, :], start=True, stop=True).then_inc(mm, 1)

                @block.vector
                def _(dve):
                    for n, (dst, src) in enumerate([
                            (uqT[:, :], BK[0][0:QL, 0:P]), (woT[:, :], BK[1][:, 0:P]),
                            (WqT[:, :], BK[3][:, 0:P]), (Wq_s[:, :], BK[4][:, 0:P]),
                            (ve[:, :], BK[5][0:QL, 0:P]), (keT[:, :], BK[6][0:QL, 0:P]),
                            (Wv_s[:, :], BK[0][:, 0:P]), (Wk_s[:, :], BK[1][:, 0:P])]):
                        dve.wait_ge(mm, [1, 2, 4, 5, 6, 7, 8, 9][n])
                        nc.vector.tensor_copy(dst, src).then_inc(copied, 1)
                    dve.wait_ge(loaded, NL)
                    for l in range(DEPTH):
                        for c in range(3):
                            j = l * 6 + c
                            nc.vector.tensor_tensor(b1_s[0:HCS[c], l, :, c], BK[2][0:HCS[c], j:j + 4:3],
                                                    b1raw[0:HCS[c], l, :, c], ALU.add)
                        nc.vector.tensor_scalar(w1_s[:, l, :], w1_s[:, l, :], lng[:, l:l + 1], None, ALU.mult)
                        tab = cst[:, 0:ROPE].rearrange("p (t f d) -> p t f d", t=NT, f=4)
                        for f in range(4):
                            sc = qs[:, l, f // 2, :]
                            if f % 2:
                                for hf in range(2):
                                    other = sc[:, (1 - hf) * 32:(1 - hf) * 32 + 32]
                                    nc.vector.tensor_tensor(
                                        ropet[:, l, :, f, hf * 32:hf * 32 + 32], tab[:, :, f, hf * 32:hf * 32 + 32],
                                        other.unsqueeze(1).to_broadcast([P, NT, 32]), ALU.mult)
                            else:
                                nc.vector.tensor_tensor(ropet[:, l, :, f, :], tab[:, :, f, :],
                                                        sc.unsqueeze(1).to_broadcast([P, NT, DH]), ALU.mult)
                    nc.vector.tensor_copy(maskb[:, :, :], cst[:, ROPE:ROPE + 3 * P].rearrange("p (a b) -> p a b", a=3))
                    nc.vector.tensor_copy(identb[:, :], ident)
            stack.pop()
            end_phase([loaded, preset, mm, copied])

        def norm_phase(first, it):
            with ExitStack() as scope:
                stack.append(scope)
                x_in = sem("x_in"); var_ok = sem("var_ok"); rstd_ok = sem("rstd_ok"); st = sem("st"); done = sem("done")
                with nc.Block() as block:
                    @block.sync
                    def _(sp):
                        if first:
                            for b in range(NB):
                                sp.dma_start(X[:, b * NT:(b + 1) * NT, :],
                                             x[it * NB + b].rearrange("(t p) c -> p t c", p=P)).then_inc(x_in, 16)

                    @block.gpsimd
                    def _(pool):
                        pool.wait_ge(var_ok, 1)
                        nc.gpsimd.tensor_tensor(rstd[:, :], rstd[:, :], mhalf[:, 0:NS], ALU.pow).then_inc(rstd_ok, 1)

                    @block.vector
                    def _(dve):
                        if first:
                            dve.wait_ge(x_in, 16 * NB)
                        for s in range(NS):
                            nc.vector.bn_stats(stats[:, s, :], X[:, s, :]).then_inc(st, 1)
                        for s in range(NS):
                            dve.wait_ge(st, s + 1)
                            nc.vector.bn_aggr(mv[:, s, :], stats[:, s, :]).then_inc(st, 1)
                        dve.wait_ge(st, 2 * NS)
                        nc.vector.tensor_scalar(rstd[:, :], mv[:, :, 1], EPS, None, ALU.add).then_inc(var_ok, 1)
                        dve.wait_ge(rstd_ok, 1)
                        for s in range(NS):
                            nc.vector.tensor_scalar(U[:, s, :], X[:, s, :], mv[:, s, 0:1], rstd[:, s:s + 1],
                                                    ALU.subtract, ALU.mult).then_inc(done, 1)
                stack.pop()
                end_phase([x_in, var_ok, rstd_ok, st, done])

        def ffn_phase():
            with ExitStack() as scope:
                stack.append(scope)
                HT = sb("HT", [P, NB, T + 1])
                HT2 = sb("HT2", [P, NB, T + 1])
                RA = sb("RA", [P, 2, 2, NH, DH])
                RB = sb("RB", [P, 2, NH, DH])
                SQ = sb("SQ", [P, 2 * NH, DH])
                SS = sb("SS", [P, 2 * NH])
                RN = sb("RN", [P, 2, 2 * NH])
                QZ = sb("QZ", [P, NH, P])
                KT = sb("KT", [P, CH, NB, W + T])
                VB = sb("VB", [P, NB, NT, NH, DH + 1])
                VA = sb("VA", [P, NB, NT, NH, DH + 1])
                PR = sb("PR", [P, NH, P])
                PT = sb("PT", [P, NH, P])
                NMX = sb("NMX", [P, NH])
                RS = sb("RS", [P, NH])
                ON = sb("ON", [P, NH, DH])
                OT = sb("OT", [P, CH, P])
                U2 = sb("U2", [P, 2, P])
                U2B = sb("U2B", [P, 2, P])
                DT = sb("DT", [P, P]); SQ2 = sb("SQ2", [P, P]); DG_ = sb("DG_", [P, P]); HN = sb("HN", [P, P])
                VE = sb("VE", [P, 1]); RV = sb("RV", [P, 1])
                GL = sb("GL", [HC, 3, P]); GLU = sb("GLU", [HC, 3, P])

                S = {n: sem(n) for n in (
                    "preset uT_in u2T_in ht_ok ht2_ok q_in k_in v_in kmul qmul ksq sq_ok ss_ok sum_ok rn_ok rot_ok "
                    "qT_in kT_in qz_ok kt_ok s_in nmx_ok p_ok pt0_in pt1_in pt0_ok pt1_ok vb_ok va_ok o_in on_ok "
                    "ot_in ot_ok wo_in u2_ok u2b_ok mean_in dt_ok sq2_ok var_in ve_ok rv_ok dg_ok bc_in hn_ok "
                    "w1a_in w1g_in gl_ok glu_ok w2_in u3_ok dch pch").split()}
                NU = DEPTH * NS
                STEPS = range(NU + 3)

                def unit(n):
                    s = n % NS
                    return n // NS, s // NT, s % NT, s

                def live(n):
                    return 0 <= n < NU

                with nc.Block() as block:
                    @block.tensor
                    def _(pe):
                        readers = [None] * 8

                        def claim(k, name, count):
                            if readers[k]:
                                pe.wait_ge(*readers[k])
                            readers[k] = (S[name], count)

                        pe.wait_ge(S["preset"], 6)
                        for n in STEPS:
                            a, b, c, d = n, n - 1, n - 2, n - 3
                            if live(b):
                                pe.wait_ge(S["rot_ok"], 2 * b + 1)
                                claim(3, "qz_ok", b + 1)
                                for j in range(CH):
                                    last = pe.transpose(BK[3][:, j * P:(j + 1) * P],
                                                        RA[:, b % 2, 0, 2 * j:2 * j + 2, :], ident)
                                last.then_inc(S["qT_in"], 1)
                                pe.wait_ge(S["rot_ok"], 2 * b + 2)
                                claim(4, "kt_ok", b + 1)
                                for j in range(CH):
                                    last = pe.transpose(BK[4][:, j * P:(j + 1) * P],
                                                        RA[:, b % 2, 1, 2 * j:2 * j + 2, :], ident)
                                last.then_inc(S["kT_in"], 1)
                            if live(a):
                                if a >= NS:
                                    pe.wait_ge(S["u3_ok"], a - NS + 1)
                                claim(5, "ht_ok", a + 1)
                                pe.transpose(BK[5][:, 0:P], U[:, unit(a)[3], :], ident).then_inc(S["uT_in"], 1)
                            if live(d):
                                pe.wait_ge(S["u2_ok"], d + 1)
                                claim(6, "ht2_ok", d + 1)
                                pe.transpose(BK[6][:, 0:P], U2[:, d % 2, :], ident).then_inc(S["u2T_in"], 1)
                            if live(c):
                                l, bb, t, s = unit(c)
                                pe.wait_ge(S["pt0_ok"], c + 1)
                                pe.wait_ge(S["pt1_ok"], c + 1)
                                pe.wait_ge(S["va_ok"], c + 1)
                                claim(7, "on_ok", 2 * c + 1)
                                claim(3, "on_ok", 2 * c + 2)
                                for h in range(NH):
                                    for w in range(2):
                                        V = (VA, VB)[w]
                                        o = (h % 4) * (DH + 1)
                                        last = nc.tensor.matmul(
                                            BK[(7, 3)[h // 4]][w * W:(w + 1) * W, o:o + DH + 1],
                                            PT[:, h, w * W:(w + 1) * W], V[:, bb, t, h, :], start=True, stop=True)
                                last.then_inc(S["o_in"], 1)
                            if live(d):
                                l, bb, t, s = unit(d)
                                pe.wait_ge(S["ht2_ok"], d + 1)
                                claim(6, "dt_ok", d + 1)
                                nc.tensor.matmul(BK[6][:, 0:P], meanw[:, :], HT2[:, bb, t * P:(t + 1) * P],
                                                 start=True, stop=True).then_inc(S["mean_in"], 1)
                            if live(a):
                                l, bb, t, s = unit(a)
                                pe.wait_ge(S["ht_ok"], a + 1)
                                for k, name, read in ((2, "v_in", "vb_ok"), (1, "k_in", "kmul"), (0, "q_in", "sq_ok")):
                                    claim(k, read, a + 1)
                                    nc.tensor.matmul(BK[k][:, :], HT[:, bb, t * P:(t + 1) * P],
                                                     wqkv_s[:, l, k * 512:(k + 1) * 512],
                                                     start=True, stop=True).then_inc(S[name], 1)
                            if live(c):
                                pe.wait_ge(S["on_ok"], 2 * c + 2)
                                claim(4, "ot_ok", c + 1)
                                for j in range(CH):
                                    last = pe.transpose(BK[4][:, j * P:(j + 1) * P], ON[:, 2 * j:2 * j + 2, :], ident)
                                last.then_inc(S["ot_in"], 1)
                            if live(d):
                                pe.wait_ge(S["sq2_ok"], d + 1)
                                claim(6, "ve_ok", d + 1)
                                nc.tensor.matmul(BK[6][:, 0:1], SQ2[:, :], meanw[:, 0:1],
                                                 start=True, stop=True).then_inc(S["var_in"], 1)
                            if live(b):
                                l, bb, t, s = unit(b)
                                pe.wait_ge(S["qz_ok"], b + 1)
                                pe.wait_ge(S["kt_ok"], b + 1)
                                claim(5, "p_ok", b + 1)
                                claim(3, "p_ok", b + 1)
                                for g in range(2):
                                    nc.tensor.matmul(BK[(5, 3)[g]][:, :].rearrange("p (a b) -> p a b", a=4), identb[:, :],
                                                     maskb[:, 1 if t == 0 else 0, :].unsqueeze(1).to_broadcast([P, 4, P]),
                                                     start=True, stop=False, skip_group_check=True)
                                for h in range(NH):
                                    for w in range(2):
                                        k0 = (2 * t + w) * W
                                        last = nc.tensor.matmul(
                                            BK[(5, 3)[h // 4]][w * W:(w + 1) * W, (h % 4) * P:(h % 4 + 1) * P],
                                            QZ[:, h, w * W:(w + 1) * W], KT[:, h // 2, bb, k0:k0 + 2 * W],
                                            start=False, stop=True, skip_group_check=True)
                                last.then_inc(S["s_in"], 1)
                            if live(c):
                                l, bb, t, s = unit(c)
                                pe.wait_ge(S["ot_ok"], c + 1)
                                claim(7, "u2_ok", c + 1)
                                for j in range(CH):
                                    last = nc.tensor.matmul(BK[7][:, 0:P], OT[:, j, :], wo_s[:, l, j, :],
                                                            start=(j == 0), stop=(j == CH - 1))
                                last.then_inc(S["wo_in"], 1)
                            if live(d):
                                l, bb, t, s = unit(d)
                                pe.wait_ge(S["dg_ok"], d + 1)
                                claim(6, "hn_ok", d + 1)
                                nc.tensor.matmul(BK[6][:, 0:P], ones[:, :], DG_[:, :],
                                                 start=True, stop=True).then_inc(S["bc_in"], 1)
                                pe.wait_ge(S["hn_ok"], d + 1)
                                for e, k, name, read in ((1, 1, "w1g_in", "gl_ok"), (0, 2, "w1a_in", "glu_ok")):
                                    claim(k, read, d + 1)
                                    for j in range(3):
                                        o = e * HID + j * HC
                                        last = nc.tensor.matmul(BK[k][0:HCS[j], j * P:(j + 1) * P],
                                                                w1_s[:, l, o:o + HCS[j]], HN[:, :],
                                                                start=True, stop=True)
                                    last.then_inc(S[name], 1)
                            if live(b):
                                pe.wait_ge(S["p_ok"], b + 1)
                                for g, k in ((0, 4), (1, 0)):
                                    claim(k, f"pt{g}_ok", b + 1)
                                    for h in range(4):
                                        last = pe.transpose(BK[k][:, h * P:(h + 1) * P], PR[:, 4 * g + h, :], ident)
                                    last.then_inc(S[f"pt{g}_in"], 1)
                            if live(d):
                                l, bb, t, s = unit(d)
                                pe.wait_ge(S["glu_ok"], d + 1)
                                claim(7, "u3_ok", d + 1)
                                for j in range(3):
                                    last = nc.tensor.matmul(BK[7][:, 0:P], GLU[0:HCS[j], j, :], w2_s[0:HCS[j], l, j, :],
                                                            start=(j == 0), stop=(j == 2))
                                last.then_inc(S["w2_in"], 1)

                    @block.scalar
                    def _(act):
                        act.wait_ge(S["preset"], 6)
                        for n in STEPS:
                            a, b, c, d = n, n - 1, n - 2, n - 3
                            if live(b):
                                act.wait_ge(S["qT_in"], b + 1)
                                if b >= 1:
                                    act.wait_ge(S["s_in"], b)
                                for hf in range(2):
                                    src = BK[3][hf * W:(hf + 1) * W, :].rearrange("p (c q) -> p c q", c=CH)
                                    last = nc.scalar.activation(QZ[hf * W:(hf + 1) * W, hf::2, :], src, ACT.Copy)
                                last.then_inc(S["qz_ok"], 1)
                            if live(a):
                                l, bb, t, s = unit(a)
                                act.wait_ge(S["v_in"], a + 1)
                                nc.scalar.activation(VB[:, bb, t, :, 0:DH],
                                                     BK[2][:, :].rearrange("p (h d) -> p h d", h=NH),
                                                     ACT.Copy).then_inc(S["vb_ok"], 1)
                                act.wait_ge(S["k_in"], a + 1)
                                if a >= 1:
                                    act.wait_ge(S["ss_ok"], a)
                                nc.scalar.activation(SQ[:, NH:2 * NH, :], BK[1][:, :].rearrange("p (h d) -> p h d", h=NH),
                                                     ACT.Square).then_inc(S["ksq"], 1)
                                act.wait_ge(S["qmul"], a + 1)
                                nc.scalar.activation(SQ[:, 0:NH, :], BK[0][:, :].rearrange("p (h d) -> p h d", h=NH),
                                                     ACT.Square).then_inc(S["sq_ok"], 1)
                            if live(d):
                                act.wait_ge(S["dt_ok"], d + 1)
                                nc.scalar.activation(SQ2[:, :], DT[:, :], ACT.Square).then_inc(S["sq2_ok"], 1)
                            if live(c):
                                act.wait_ge(S["ot_in"], c + 1)
                                nc.scalar.activation(OT[:, :, :], BK[4][:, :].rearrange("p (c q) -> p c q", c=CH),
                                                     ACT.Copy).then_inc(S["ot_ok"], 1)
                            if live(b):
                                act.wait_ge(S["nmx_ok"], b + 1)
                                for h in range(NH):
                                    last = nc.scalar.activation(PR[:, h, :], BK[(5, 3)[h // 4]][:, (h % 4) * P:(h % 4 + 1) * P],
                                                                ACT.Exp, bias=NMX[:, h:h + 1], scale=8.0)
                                last.then_inc(S["p_ok"], 1)
                            if live(d):
                                l, bb, t, s = unit(d)
                                act.wait_ge(S["w1g_in"], d + 1)
                                for j in range(3):
                                    last = nc.scalar.activation(GL[0:HCS[j], j, :], BK[1][0:HCS[j], j * P:(j + 1) * P],
                                                                ACT.Gelu, bias=b1_s[0:HCS[j], l, 1, j:j + 1])
                                last.then_inc(S["gl_ok"], 1)
                            if live(b):
                                act.wait_ge(S["pt1_in"], b + 1)
                                nc.scalar.activation(PT[:, 4:8, :], BK[0][:, :].rearrange("p (h q) -> p h q", h=4),
                                                     ACT.Copy).then_inc(S["pt1_ok"], 1)

                    @block.vector
                    def _(dve):
                        chain = [0]

                        def link(ins):
                            chain[0] += 1
                            ins.then_inc(S["dch"], 1)
                            dve.wait_ge(S["dch"], chain[0])

                        nc.vector.memset(HT[W:P, :, 0:1], 0.0).then_inc(S["preset"], 1)
                        nc.vector.memset(HT2[W:P, :, 0:1], 0.0).then_inc(S["preset"], 1)
                        nc.vector.memset(VB[:, :, :, :, DH:DH + 1], 1.0).then_inc(S["preset"], 1)
                        nc.vector.memset(KT[:, :, :, 0:W], 0.0).then_inc(S["preset"], 1)
                        nc.vector.memset(VA[0:W, :, 0, :, :], 0.0)
                        nc.vector.memset(QZ[0:W, 1::2, :], 0.0).then_inc(S["preset"], 1)
                        nc.vector.memset(QZ[W:P, 0::2, :], 0.0).then_inc(S["preset"], 1)
                        dve.wait_ge(S["preset"], 6)
                        for n in STEPS:
                            a, b, c, d = n, n - 1, n - 2, n - 3
                            if live(b):
                                l, bb, t, s = unit(b)
                                dve.wait_ge(S["kT_in"], b + 1)
                                nc.vector.tensor_copy(KT[:, :, bb, W + t * P:W + (t + 1) * P],
                                                           BK[4][:, :].rearrange("p (c q) -> p c q", c=CH)).then_inc(S["kt_ok"], 1)
                            for m, src, dst, inn, okk, k in ((a, 5, HT, "uT_in", "ht_ok", 5), (d, 6, HT2, "u2T_in", "ht2_ok", 6)):
                                if live(m):
                                    l, bb, t, s = unit(m)
                                    dve.wait_ge(S[inn], m + 1)
                                    nc.vector.tensor_copy(dst[0:W, bb, t * P:(t + 1) * P], BK[src][0:W, 0:P])
                                    nc.vector.tensor_copy(dst[W:P, bb, t * P + 1:(t + 1) * P + 1], BK[src][W:P, 0:P]).then_inc(S[okk], 1)
                            if live(c):
                                dve.wait_ge(S["o_in"], c + 1)
                                if c >= 1:
                                    dve.wait_ge(S["ot_in"], c)
                                for g, k in ((0, 7), (1, 3)):
                                    O = BK[k][:, 0:4 * (DH + 1)].rearrange("p (h d) -> p h d", h=4)
                                    link(nc.vector.reciprocal(RS[:, 4 * g:4 * g + 4], O[:, :, DH]))
                                    nc.vector.tensor_tensor(ON[:, 4 * g:4 * g + 4, :], O[:, :, 0:DH],
                                                                 RS[:, 4 * g:4 * g + 4].unsqueeze(2).to_broadcast([P, 4, DH]),
                                                                 ALU.mult).then_inc(S["on_ok"], 1)
                            if live(d):
                                l, bb, t, s = unit(d)
                                dve.wait_ge(S["mean_in"], d + 1)
                                if d >= 1:
                                    dve.wait_ge(S["sq2_ok"], d)
                                nc.vector.scalar_tensor_tensor(
                                        out=DT[:, :], in0=BK[6][:, 0:P], scalar=-1.0, in1=HT2[:, bb, t * P:(t + 1) * P],
                                        op0=ALU.mult, op1=ALU.add).then_inc(S["dt_ok"], 1)
                            if live(a):
                                l, bb, t, s = unit(a)
                                for e, k in ((0, 0), (1, 1)):
                                    dve.wait_ge(S[("q_in", "k_in")[e]], a + 1)
                                    if e == 1:
                                        dve.wait_ge(S["ksq"], a + 1)
                                    if a >= 2 and e == 0:
                                        dve.wait_ge(S["kT_in"], a - 1)
                                    if a >= 1:
                                        dve.wait_ge(S["sum_ok"], 2 * a - 1 + e)
                                    src = BK[k][:, :].rearrange("p (h d) -> p h d", h=NH)
                                    rot = BK[k][:, :].rearrange("p (h z d) -> p h z d", h=NH, z=2)[:, :, ::-1, :]
                                    nc.vector.tensor_tensor(RA[:, a % 2, e, :, :], src,
                                                            ropet[:, l, t, 2 * e, :].unsqueeze(1).to_broadcast([P, NH, DH]),
                                                            ALU.mult)
                                    tab = ropet[:, l, t, 2 * e + 1, :].rearrange("p (z d) -> p z d", z=2)
                                    nc.vector.tensor_tensor(
                                        RB[:, e, :, :].rearrange("p h (z d) -> p h z d", z=2), rot,
                                        tab.unsqueeze(1).to_broadcast([P, NH, 2, 32]), ALU.mult).then_inc(S[("qmul", "kmul")[e]], 1)
                                dve.wait_ge(S["sq_ok"], a + 1)
                                if a >= 1:
                                    dve.wait_ge(S["rn_ok"], a)
                                link(nc.vector.tensor_reduce(SS[:, :], SQ[:, :, :], AX_X, ALU.add))
                                nc.vector.tensor_scalar(SS[:, :], SS[:, :], 1e-24, None, ALU.max).then_inc(S["ss_ok"], 1)
                            if live(d):
                                dve.wait_ge(S["var_in"], d + 1)
                                nc.vector.tensor_scalar(VE[:, :], BK[6][:, 0:1], EPS, None, ALU.add).then_inc(S["ve_ok"], 1)
                                dve.wait_ge(S["rv_ok"], d + 1)
                                nc.vector.tensor_scalar(DG_[:, :], ident, RV[:, 0:1], None, ALU.mult).then_inc(S["dg_ok"], 1)
                            if live(b):
                                dve.wait_ge(S["s_in"], b + 1)
                                for g, k in ((0, 5), (1, 3)):
                                    last = nc.vector.tensor_reduce(NMX[:, 4 * g:4 * g + 4],
                                                                   BK[k][:, :].rearrange("p (h q) -> p h q", h=4), AX_X, ALU.max)
                                link(last)
                                nc.vector.tensor_scalar(NMX[:, :], NMX[:, :], -8.0, None, ALU.mult).then_inc(S["nmx_ok"], 1)
                            if live(a):
                                l, bb, t, s = unit(a)
                                dve.wait_ge(S["vb_ok"], a + 1)
                                if t < NT - 1:
                                    nc.vector.tensor_copy(VA[0:W, bb, t + 1, :, :], VB[W:P, bb, t, :, :])
                                nc.vector.tensor_copy(VA[W:P, bb, t, :, :], VB[0:W, bb, t, :, :]).then_inc(S["va_ok"], 1)
                            if live(d):
                                dve.wait_ge(S["bc_in"], d + 1)
                                nc.vector.tensor_tensor(HN[:, :], BK[6][:, 0:P], DT[:, :], ALU.mult).then_inc(S["hn_ok"], 1)
                            if live(c):
                                l, bb, t, s = unit(c)
                                dve.wait_ge(S["wo_in"], c + 1)
                                nc.vector.tensor_tensor(U2[:, c % 2, :], BK[7][:, 0:P], U[:, s, :], ALU.add).then_inc(S["u2_ok"], 1)
                            if live(d):
                                l, bb, t, s = unit(d)
                                dve.wait_ge(S["w1a_in"], d + 1)
                                dve.wait_ge(S["gl_ok"], d + 1)
                                if d >= 1:
                                    dve.wait_ge(S["w2_in"], d)
                                for j in range(3):
                                    h_ = HCS[j]
                                    last = nc.vector.scalar_tensor_tensor(
                                        out=GLU[0:h_, j, :], in0=BK[2][0:h_, j * P:(j + 1) * P],
                                        scalar=b1_s[0:h_, l, 0, j:j + 1], in1=GL[0:h_, j, :], op0=ALU.add, op1=ALU.mult)
                                last.then_inc(S["glu_ok"], 1)
                            if live(b):
                                dve.wait_ge(S["pt0_in"], b + 1)
                                nc.vector.tensor_copy(PT[:, 0:4, :], BK[4][:, :].rearrange("p (h q) -> p h q", h=4)).then_inc(S["pt0_ok"], 1)
                            if live(d):
                                l, bb, t, s = unit(d)
                                dve.wait_ge(S["w2_in"], d + 1)
                                dve.wait_ge(S["u2b_ok"], d + 1)
                                nc.vector.tensor_tensor(U[:, s, :], BK[7][:, 0:P], U2B[:, d % 2, :],
                                                        ALU.add).then_inc(S["u3_ok"], 1)
                                if l == DEPTH - 1:
                                    dve.wait_ge(S["u3_ok"], d + 1)
                                    nc.vector.scalar_tensor_tensor(out=X[:, s, :], in0=U[:, s, :], scalar=0.5,
                                                                   in1=X[:, s, :], op0=ALU.mult, op1=ALU.add)

                    @block.gpsimd
                    def _(pool):
                        for n in STEPS:
                            a, b, c, d = n, n - 1, n - 2, n - 3
                            if live(a):
                                for e in range(2):
                                    pool.wait_ge(S[("qmul", "kmul")[e]], a + 1)
                                    nc.gpsimd.tensor_tensor(RA[:, a % 2, e, :, :], RA[:, a % 2, e, :, :], RB[:, e, :, :],
                                                            ALU.add).then_inc(S["sum_ok"], 1)
                            if live(d):
                                pool.wait_ge(S["ve_ok"], d + 1)
                                if d >= 1:
                                    pool.wait_ge(S["dg_ok"], d)
                                nc.gpsimd.tensor_tensor(RV[:, :], VE[:, :], mhalf[:, 0:1], ALU.pow).then_inc(S["rv_ok"], 1)
                            if live(a):
                                pool.wait_ge(S["ss_ok"], a + 1)
                                nc.gpsimd.tensor_tensor(RN[:, a % 2, :], SS[:, :], mhalf[:, 0:2 * NH], ALU.pow).then_inc(S["rn_ok"], 1)
                                pool.wait_ge(S["rn_ok"], a + 1)
                                pool.wait_ge(S["sum_ok"], 2 * a + 2)
                                for e in range(2):
                                    nc.gpsimd.tensor_tensor(RA[:, a % 2, e, :, :], RA[:, a % 2, e, :, :],
                                                            RN[:, a % 2, e * NH:(e + 1) * NH].unsqueeze(2).to_broadcast([P, NH, DH]),
                                                            ALU.mult).then_inc(S["rot_ok"], 1)
                            if live(c):
                                l, bb, t, s = unit(c)
                                pool.wait_ge(S["u2_ok"], c + 1)
                                nc.gpsimd.tensor_tensor(U2B[:, c % 2, :], U2[:, c % 2, :], b2_s[:, l, :], ALU.add).then_inc(S["u2b_ok"], 1)
                stack.pop()
                end_phase(list(S.values()))

        def mla_phase():
            with ExitStack() as scope:
                stack.append(scope)
                XT = sb("XT", [P, T]); QT = sb("QT", [P, T]); KL = sb("KL", [P, T])
                QZL = sb("QZL", [P, NG, T])
                VL = sb("VL", [P, NT, NG, 32])
                PL = sb("PL", [P, 3, T])
                PTL = sb("PTL", [P, 2, LG, NT, T])
                OTL = sb("OTL", [P, T])
                RL = sb("RL", [P, NT, LG])
                Y = sb("Y", [P, NT, LG, DG])
                NM = sb("NM", [P, 4])
                S = {n: sem(n) for n in (
                    "preset xt_in xt_ok q_in k_in v_in qt_ok kl_ok vl_ok qz_ok s_in nm_ok p_ok pt_in pt_ok o_in "
                    "ot_ok y_in y_ok pv_done dch").split()}
                NM_UNITS = NG * NT
                SCALE = float(DG) ** -0.5
                GROUPS = NG // LG
                PER = NT * LG

                def munit(m):
                    g, r = divmod(m, PER)
                    i, hh = divmod(r, LG)
                    return g, i, hh, g * LG + hh

                def evac(eng, ops, S, bb, M0, k):
                    g, i, hh, h = munit(k)
                    kk = M0 + k
                    eng.wait_ge(S["pt_in"], kk + 1)
                    if kk >= 2 * PER:
                        eng.wait_ge(S["o_in"], kk // PER - 1)
                    if kk >= 1:
                        eng.wait_ge(S["pt_ok"], kk)
                    dst = PTL[:, kk // PER % 2, hh, 0:i + 1, i * P:(i + 1) * P]
                    src = BK[4 + kk % 2][:, 0:(i + 1) * P].rearrange("p (j q) -> p j q", q=P)
                    if k % 2:
                        ops.activation(dst, src, ACT.Copy).then_inc(S["pt_ok"], 1)
                    else:
                        ops.tensor_copy(dst, src).then_inc(S["pt_ok"], 1)

                with nc.Block() as block:
                    @block.tensor
                    def _(pe):
                        pe.wait_ge(S["preset"], 1)
                        for bb in range(NB):
                            M0 = bb * NM_UNITS
                            G0 = bb * GROUPS
                            if bb:
                                pe.wait_ge(S["y_ok"], G0)
                            for t in range(NT):
                                last = pe.transpose(BK[7][:, t * P:(t + 1) * P], U[:, bb * NT + t, :], ident)
                            last.then_inc(S["xt_in"], 1)
                            pe.wait_ge(S["xt_ok"], bb + 1)
                            if bb:
                                pe.wait_ge(S["p_ok"], M0)
                            nc.tensor.matmul(BK[0][:, :], Wq_s[:, :], XT[:, :], start=True, stop=True).then_inc(S["q_in"], 1)
                            nc.tensor.matmul(BK[1][:, :], Wk_s[:, :], XT[:, :], start=True, stop=True).then_inc(S["k_in"], 1)
                            for t in range(NT):
                                last = nc.tensor.matmul(BK[2][:, t * P:(t + 1) * P], XT[:, t * P:(t + 1) * P], Wv_s[:, :],
                                                        start=True, stop=True)
                            last.then_inc(S["v_in"], 1)
                            pe.wait_ge(S["qt_ok"], bb + 1)
                            pe.wait_ge(S["kl_ok"], bb + 1)
                            pe.wait_ge(S["vl_ok"], bb + 1)
                            for m in range(NM_UNITS + 8):
                                if m < NM_UNITS:
                                    g, i, hh, h = munit(m)
                                    mm_ = M0 + m
                                    if i == 0:
                                        pe.wait_ge(S["qz_ok"], bb * NG + h + 1)
                                    if m >= 4:
                                        pe.wait_ge(S["p_ok"], mm_ - 3)
                                    bk = BK[mm_ % 4]
                                    N = (i + 1) * P
                                    nc.tensor.matmul(bk[:, 0:N], QZL[:, h, i * P:(i + 1) * P], KL[:, 0:N],
                                                     start=True, stop=False, skip_group_check=True)
                                    nc.tensor.matmul(bk[:, i * P:N], identb[:, :], maskb[:, 2, :],
                                                     start=False, stop=True, skip_group_check=True).then_inc(S["s_in"], 1)
                                if 2 <= m < NM_UNITS + 2:
                                    k = m - 2
                                    g, i, hh, h = munit(k)
                                    kk = M0 + k
                                    pe.wait_ge(S["p_ok"], kk + 1)
                                    if kk >= 2:
                                        pe.wait_ge(S["pt_ok"], kk - 1)
                                    for j in range(i + 1):
                                        last = pe.transpose(BK[4 + kk % 2][:, j * P:(j + 1) * P],
                                                            PL[:, kk % 3, j * P:(j + 1) * P], ident)
                                    last.then_inc(S["pt_in"], 1)
                                k = m - 4
                                if k >= 0 and k % PER == PER - 1:
                                    g = k // PER
                                    gg = G0 + g
                                    pe.wait_ge(S["pt_ok"], M0 + k + 1)
                                    if gg >= 1:
                                        pe.wait_ge(S["ot_ok"], gg)
                                    for j in range(NT):
                                        for q in range(LG):
                                            last = nc.tensor.matmul(BK[6][32 * q:32 * q + 32, j * P:T],
                                                                    VL[:, j, g * LG + q, :], PTL[:, gg % 2, q, j, j * P:T],
                                                                    start=(j == 0), stop=(j == NT - 1),
                                                                    skip_group_check=True)
                                    last.then_inc(S["o_in"], 1)
                                k = m - 6
                                if k >= 0 and k % PER == PER - 1:
                                    gg = G0 + k // PER
                                    pe.wait_ge(S["ot_ok"], gg + 1)
                                    if gg >= 1:
                                        pe.wait_ge(S["y_ok"], gg)
                                    for t in range(NT):
                                        last = pe.transpose(BK[7][:, t * P:(t + 1) * P], OTL[:, t * P:(t + 1) * P], ident)
                                    last.then_inc(S["y_in"], 1)

                    @block.scalar
                    def _(act):
                        act.wait_ge(S["preset"], 1)
                        for bb in range(NB):
                            M0, G0 = bb * NM_UNITS, bb * GROUPS
                            act.wait_ge(S["v_in"], bb + 1)
                            nc.scalar.activation(VL[:, :, :, 0:DG], BK[2][:, :].rearrange("p (t h d) -> p t h d", t=NT, h=NG),
                                                 ACT.Copy).then_inc(S["vl_ok"], 1)
                            for m in range(NM_UNITS + 8):
                                if m < NM_UNITS:
                                    g, i, hh, h = munit(m)
                                    mm_ = M0 + m
                                    N = (i + 1) * P
                                    act.wait_ge(S["nm_ok"], mm_ + 1)
                                    if mm_ >= 3:
                                        act.wait_ge(S["pt_in"], mm_ - 2)
                                    nc.scalar.activation(PL[:, mm_ % 3, 0:N], BK[mm_ % 4][:, 0:N], ACT.Exp,
                                                         bias=NM[:, mm_ % 4:mm_ % 4 + 1], scale=SCALE).then_inc(S["p_ok"], 1)
                                k = m - 3
                                if 0 <= k < NM_UNITS and k % 2 == 1:
                                    evac(act, nc.scalar, S, bb, M0, k)

                    @block.vector
                    def _(dve):
                        chain = [0]

                        def link(ins):
                            chain[0] += 1
                            ins.then_inc(S["dch"], 1)
                            dve.wait_ge(S["dch"], chain[0])

                        link(nc.vector.memset(VL[:, :, :, :], 0.0))
                        nc.vector.memset(VL[:, :, :, DG:DG + 1], 1.0).then_inc(S["preset"], 1)
                        dve.wait_ge(S["preset"], 1)
                        for bb in range(NB):
                            M0, G0 = bb * NM_UNITS, bb * GROUPS
                            dve.wait_ge(S["xt_in"], bb + 1)
                            nc.vector.tensor_copy(XT[:, :], BK[7][:, :]).then_inc(S["xt_ok"], 1)
                            dve.wait_ge(S["q_in"], bb + 1)
                            nc.vector.tensor_copy(QT[:, :], BK[0][:, :]).then_inc(S["qt_ok"], 1)
                            dve.wait_ge(S["k_in"], bb + 1)
                            nc.vector.tensor_copy(KL[:, :], BK[1][:, :]).then_inc(S["kl_ok"], 1)
                            dve.wait_ge(S["qt_ok"], bb + 1)
                            for h in range(NG):
                                nc.vector.tensor_scalar(QZL[:, h, :], QT[:, :], headsel[:, h:h + 1], None,
                                                        ALU.mult).then_inc(S["qz_ok"], 1)
                            for m in range(NM_UNITS + 8):
                                if m < NM_UNITS:
                                    g, i, hh, h = munit(m)
                                    mm_ = M0 + m
                                    N = (i + 1) * P
                                    dve.wait_ge(S["s_in"], mm_ + 1)
                                    if mm_ >= 4:
                                        dve.wait_ge(S["p_ok"], mm_ - 3)
                                    c = NM[:, mm_ % 4:mm_ % 4 + 1]
                                    link(nc.vector.tensor_reduce(c, BK[mm_ % 4][:, 0:N], AX_X, ALU.max))
                                    nc.vector.tensor_scalar(c, c, -SCALE, None, ALU.mult).then_inc(S["nm_ok"], 1)
                                k = m - 3
                                if 0 <= k < NM_UNITS and k % 2 == 0:
                                    evac(dve, nc.vector, S, bb, M0, k)
                                k = m - 5
                                if k >= 0 and k % PER == PER - 1:
                                    gg = G0 + k // PER
                                    dve.wait_ge(S["o_in"], gg + 1)
                                    if gg >= 1:
                                        dve.wait_ge(S["y_in"], gg)
                                    nc.vector.tensor_copy(OTL[:, :], BK[6][:, :]).then_inc(S["ot_ok"], 1)
                                k = m - 7
                                if k >= 0 and k % PER == PER - 1:
                                    g = k // PER
                                    gg = G0 + g
                                    dve.wait_ge(S["y_in"], gg + 1)
                                    O = BK[7][:, :].rearrange("p (t h d) -> p t h d", t=NT, h=LG)
                                    link(nc.vector.reciprocal(RL[:, :, :], O[:, :, :, DG]))
                                    nc.vector.tensor_tensor(Y[:, :, :, :], O[:, :, :, 0:DG],
                                                                 RL[:, :, :].unsqueeze(3).to_broadcast([P, NT, LG, DG]),
                                                                 ALU.mult).then_inc(S["y_ok"], 1)
                                    dve.wait_ge(S["y_ok"], gg + 1)
                                    xs = X[:, bb * NT:(bb + 1) * NT, g * LG * DG:(g + 1) * LG * DG]
                                    link(nc.vector.tensor_tensor(xs, xs, Y[:, :, :, :].rearrange("p t h d -> p t (h d)"), ALU.add))
                stack.pop()
                end_phase(list(S.values()))

        with nc.Fori(0, B // NB, 1) as it:
            norm_phase(True, it)
            ffn_phase()
            norm_phase(False, it)
            mla_phase()
            norm_phase(False, it)
            ffn_phase()
            stored = sem("stored")
            with nc.Block() as block:
                @block.sync
                def _(sp):
                    for b in range(NB):
                        sp.dma_start(out[it * NB + b].rearrange("(t p) c -> p t c", p=P),
                                     X[:, b * NT:(b + 1) * NT, :]).then_inc(stored, 16)
                    sp.wait_ge(stored, 16 * NB)
            end_phase([stored])


_INS = ["L0_attn_x", "L0_attn_W_dq", "L0_attn_W_uq", "L0_attn_W_dkv", "L0_attn_W_uk", "L0_attn_W_uv", "L0_attn_W_o",
        "L0_ffn_wqkv", "L0_ffn_q_scale", "L0_ffn_k_scale", "L0_ffn_wo", "L0_ffn_ln_g", "L0_ffn_ln_b", "L0_ffn_w1",
        "L0_ffn_b1", "L0_ffn_w2", "L0_ffn_b2"]


def kernel(**inputs):
    import numpy as _np
    import concourse.bacc as _bacc
    from concourse import mybir as _mybir
    from concourse.bass_utils import run_bass_kernel_spmd as _run

    nc = _bacc.Bacc("TRN2", target_bir_lowering=False, num_devices=1)
    arrays, args = {}, []
    for name in _INS:
        a = _np.ascontiguousarray(inputs[name])
        arrays[f"in_{name}"] = a
        args.append(nc.dram_tensor(f"in_{name}", a.shape, _mybir.dt.from_np(a.dtype), kind="ExternalInput").ap())
    shape = tuple(inputs["L0_attn_x"].shape)
    c = shape_constants(shape[1])
    arrays["shape_constants"] = c
    args.append(nc.dram_tensor("shape_constants", c.shape, F32, kind="ExternalInput").ap())
    args.append(nc.dram_tensor("out_0", shape, F32, kind="ExternalOutput").ap())
    macaron(nc, *args)
    r = _run(nc, [arrays], core_ids=[0])
    return r.results[0]["out_0"]
```

```python
from contextlib import ExitStack

import numpy as np
import concourse.bass as bass
from concourse import mybir

F32 = mybir.dt.float32
BF16 = mybir.dt.bfloat16
ALU = mybir.AluOpType
ACT = mybir.ActivationFunctionType
AX_X = mybir.AxisListType.X

P = 128
W = 64
NH, DH = 8, 64
NG, DG = 16, 8
EPS = 1e-5
BIG = -1e30
LG = 4


def shape_constants(T):
    half = np.arange(0, DH, 2, dtype=np.float32)
    inv = (1.0 / np.float32(10000.0) ** (half / np.float32(DH))).astype(np.float32)
    t = np.arange(T, dtype=np.float32)
    f = t[:, None] * inv[None, :]
    base = ((half + np.float32(0.4 * DH)) / np.float32(1.4 * DH)).astype(np.float32)
    power = ((t - T // 2) / np.float32(W // 2)).astype(np.float32)
    s = (base[None, :] ** power[:, None]).astype(np.float32)
    c, sn = np.cos(f), np.sin(f)
    tab = np.stack([np.concatenate([c * s, c * s], -1), np.concatenate([-sn * s, sn * s], -1),
                    np.concatenate([c / s, c / s], -1), np.concatenate([-sn / s, sn / s], -1)], 1)
    rope = tab.reshape(T // P, P, 4, DH).transpose(1, 0, 2, 3).reshape(P, -1).astype(np.float32)
    q, k = np.arange(P)[:, None] % W, np.arange(P)[None, :]
    band = np.where((k <= W + q) & (k >= q), 0.0, BIG).astype(np.float32)
    first = band.copy()
    first[:W, :W] = BIG
    causal = np.where(np.arange(P)[None, :] <= np.arange(P)[:, None], 0.0, BIG).astype(np.float32)
    headsel = (np.arange(P)[:, None] // DG == np.arange(NG)[None, :]).astype(np.float32)
    return np.concatenate([rope, band, first, causal, np.eye(P, dtype=np.float32), headsel], 1)


def macaron(nc, x, W_dq, W_uq, W_dkv, W_uk, W_uv, W_o, wqkv, q_scale, k_scale, wo, ln_g, ln_b,
            w1, b1, w2, b2, consts, out):
    B, T, C = x.shape
    DEPTH, HID = w2.shape[0], w2.shape[1]
    NT = T // P
    NB = 2
    NS = NB * NT
    QL = W_dq.shape[0]
    HC = -(-HID // 3)
    HCS = [HC, HC, HID - 2 * HC]
    CH = NH * DH // P
    top = ExitStack()
    with top:
        stack = [top]
        phase = [0]

        def sb(name, shape, dt=F32):
            return stack[-1].enter_context(nc.sbuf_tensor(f"{name}_{phase[0]}", shape, dt))

        def sem(name):
            return stack[-1].enter_context(nc.semaphore(f"{name}_{phase[0]}"))

        BK = [top.enter_context(nc.psum_tensor(f"bank{i}", [P, 512], F32)) for i in range(8)]

        ROPE = NT * 4 * DH
        cst = sb("cst", [P, ROPE + 4 * P + NG])
        ident = cst[:, ROPE + 3 * P:ROPE + 4 * P]
        headsel = cst[:, ROPE + 4 * P:ROPE + 4 * P + NG]
        maskb = sb("maskb", [P, 3, P], BF16)
        identb = sb("identb", [P, P], BF16)
        ropet = sb("ropet", [P, DEPTH, NT, 4, DH])
        wqkv_s = sb("wqkv_s", [P, DEPTH, 3 * NH * DH])
        wo_s = sb("wo_s", [P, DEPTH, CH, P])
        w1_s = sb("w1_s", [P, DEPTH, 2 * HID])
        w2_s = sb("w2_s", [HC, DEPTH, 3, P])
        b1_s = sb("b1_s", [HC, DEPTH, 2, 3])
        b2_s = sb("b2_s", [P, DEPTH, P])
        lng = sb("lng", [P, DEPTH])
        lnb = sb("lnb", [P, DEPTH])
        meanw = sb("meanw", [P, P])
        ones = sb("ones", [P, P])
        mhalf = sb("mhalf", [P, 2 * NH])
        Wq_s = sb("Wq_s", [P, P])
        Wk_s = sb("Wk_s", [P, P])
        Wv_s = sb("Wv_s", [P, P])
        X = sb("X", [P, NS, P])
        U = sb("U", [P, NS, P])
        stats = sb("stats", [P, NS, 6])
        mv = sb("mv", [P, NS, 2])
        rstd = sb("rstd", [P, NS])

        def end_phase(sems):
            for s in sems:
                nc.sync.sem_clear(s)
            nc.all_engine_barrier()
            phase[0] += 1

        with ExitStack() as scope:
            stack.append(scope)
            qs = sb("qs", [P, DEPTH, 2, DH])
            ks = sb("ks", [P, DEPTH, DH])
            dq = sb("dq", [QL, P]); uq = sb("uq", [P, QL]); dkv = sb("dkv", [QL, P])
            uk = sb("uk", [P, QL]); uv = sb("uv", [P, QL]); wom = sb("wom", [P, P])
            uqT = sb("uqT", [QL, P]); woT = sb("woT", [P, P]); WqT = sb("WqT", [P, P])
            keT = sb("keT", [QL, P]); ve = sb("ve", [QL, P])
            b1raw = sb("b1raw", [HC, DEPTH, 2, 3])
            loaded = sem("loaded"); preset = sem("preset"); mm = sem("mm"); copied = sem("copied")
            LOADS = [0]
            with nc.Block() as block:
                @block.sync
                def _(sp):
                    def load(dst, src):
                        sp.dma_start(dst, src).then_inc(loaded, 16)
                        LOADS[0] += 16
                    load(cst[:, :], consts)
                    load(dq[:, :], W_dq); load(uq[:, :], W_uq); load(dkv[:, :], W_dkv)
                    load(uk[:, :], W_uk); load(uv[:, :], W_uv); load(wom[:, :], W_o)
                    for l in range(DEPTH):
                        load(wqkv_s[:, l, :], wqkv[l])
                        load(wo_s[:, l, :, :], wo[l].rearrange("(c p) n -> p c n", p=P))
                        load(w1_s[:, l, :], w1[l])
                        for c in range(3):
                            load(w2_s[0:HCS[c], l, c, :], w2[l][c * HC:c * HC + HCS[c], :])
                            for e in range(2):
                                o = e * HID + c * HC
                                load(b1raw[0:HCS[c], l, e, c:c + 1],
                                     b1[l][o:o + HCS[c]].rearrange("(p a) -> p a", a=1))
                        load(b2_s[:, l, :], b2[l:l + 1, :].broadcast_to([P, P]))
                        load(qs[:, l, 0, :], q_scale[l:l + 1, :].broadcast_to([P, DH]))
                        load(qs[:, l, 1, :], k_scale[l:l + 1, :].broadcast_to([P, DH]))
                        load(lng[:, l:l + 1], ln_g[l].rearrange("(p a) -> p a", a=1))
                        load(lnb[:, l:l + 1], ln_b[l].rearrange("(p a) -> p a", a=1))
                NL = LOADS[0]

                @block.gpsimd
                def _(pool):
                    nc.gpsimd.memset(meanw[:, :], 1.0 / C).then_inc(preset, 1)
                    nc.gpsimd.memset(ones[:, :], 1.0).then_inc(preset, 1)
                    nc.gpsimd.memset(mhalf[:, :], -0.5).then_inc(preset, 1)

                @block.tensor
                def _(pe):
                    pe.wait_ge(loaded, NL)
                    pe.transpose(BK[0][0:QL, 0:P], uq[:, :], ident).then_inc(mm, 1)
                    pe.transpose(BK[1][:, 0:P], wom[:, :], ident).then_inc(mm, 1)
                    for l in range(DEPTH):
                        for e in range(2):
                            for c in range(3):
                                o = e * HID + c * HC
                                j = (l * 2 + e) * 3 + c
                                last = nc.tensor.matmul(BK[2][0:HCS[c], j:j + 1], w1_s[:, l, o:o + HCS[c]],
                                                        lnb[:, l:l + 1], start=True, stop=True)
                    last.then_inc(mm, 1)
                    pe.wait_ge(copied, 1)
                    nc.tensor.matmul(BK[3][:, 0:P], uqT[:, :], dq[:, :], start=True, stop=True).then_inc(mm, 1)
                    nc.tensor.matmul(BK[4][:, 0:P], dq[:, :], uqT[:, :], start=True, stop=True).then_inc(mm, 1)
                    pe.wait_ge(copied, 2)
                    nc.tensor.matmul(BK[5][0:QL, 0:P], uv[:, :], woT[:, :], start=True, stop=True).then_inc(mm, 1)
                    pe.wait_ge(copied, 3)
                    nc.tensor.matmul(BK[6][0:QL, 0:P], uk[:, :], WqT[:, :], start=True, stop=True).then_inc(mm, 1)
                    pe.wait_ge(copied, 5)
                    nc.tensor.matmul(BK[0][:, 0:P], dkv[:, :], ve[:, :], start=True, stop=True).then_inc(mm, 1)
                    pe.wait_ge(copied, 6)
                    nc.tensor.matmul(BK[1][:, 0:P], dkv[:, :], keT[:, :], start=True, stop=True).then_inc(mm, 1)

                @block.vector
                def _(dve):
                    for n, (dst, src) in enumerate([
                            (uqT[:, :], BK[0][0:QL, 0:P]), (woT[:, :], BK[1][:, 0:P]),
                            (WqT[:, :], BK[3][:, 0:P]), (Wq_s[:, :], BK[4][:, 0:P]),
                            (ve[:, :], BK[5][0:QL, 0:P]), (keT[:, :], BK[6][0:QL, 0:P]),
                            (Wv_s[:, :], BK[0][:, 0:P]), (Wk_s[:, :], BK[1][:, 0:P])]):
                        dve.wait_ge(mm, [1, 2, 4, 5, 6, 7, 8, 9][n])
                        nc.vector.tensor_copy(dst, src).then_inc(copied, 1)
                    dve.wait_ge(loaded, NL)
                    for l in range(DEPTH):
                        for c in range(3):
                            j = l * 6 + c
                            nc.vector.tensor_tensor(b1_s[0:HCS[c], l, :, c], BK[2][0:HCS[c], j:j + 4:3],
                                                    b1raw[0:HCS[c], l, :, c], ALU.add)
                        nc.vector.tensor_scalar(w1_s[:, l, :], w1_s[:, l, :], lng[:, l:l + 1], None, ALU.mult)
                        tab = cst[:, 0:ROPE].rearrange("p (t f d) -> p t f d", t=NT, f=4)
                        for f in range(4):
                            sc = qs[:, l, f // 2, :]
                            if f % 2:
                                for hf in range(2):
                                    other = sc[:, (1 - hf) * 32:(1 - hf) * 32 + 32]
                                    nc.vector.tensor_tensor(
                                        ropet[:, l, :, f, hf * 32:hf * 32 + 32], tab[:, :, f, hf * 32:hf * 32 + 32],
                                        other.unsqueeze(1).to_broadcast([P, NT, 32]), ALU.mult)
                            else:
                                nc.vector.tensor_tensor(ropet[:, l, :, f, :], tab[:, :, f, :],
                                                        sc.unsqueeze(1).to_broadcast([P, NT, DH]), ALU.mult)
                    nc.vector.tensor_copy(maskb[:, :, :], cst[:, ROPE:ROPE + 3 * P].rearrange("p (a b) -> p a b", a=3))
                    nc.vector.tensor_copy(identb[:, :], ident)
            stack.pop()
            end_phase([loaded, preset, mm, copied])

        def norm_phase(first, it):
            with ExitStack() as scope:
                stack.append(scope)
                x_in = sem("x_in"); var_ok = sem("var_ok"); rstd_ok = sem("rstd_ok"); st = sem("st"); done = sem("done")
                with nc.Block() as block:
                    @block.sync
                    def _(sp):
                        if first:
                            for b in range(NB):
                                sp.dma_start(X[:, b * NT:(b + 1) * NT, :],
                                             x[it * NB + b].rearrange("(t p) c -> p t c", p=P)).then_inc(x_in, 16)

                    @block.gpsimd
                    def _(pool):
                        pool.wait_ge(var_ok, 1)
                        nc.gpsimd.tensor_tensor(rstd[:, :], rstd[:, :], mhalf[:, 0:NS], ALU.pow).then_inc(rstd_ok, 1)

                    @block.vector
                    def _(dve):
                        if first:
                            dve.wait_ge(x_in, 16 * NB)
                        for s in range(NS):
                            nc.vector.bn_stats(stats[:, s, :], X[:, s, :]).then_inc(st, 1)
                        for s in range(NS):
                            dve.wait_ge(st, s + 1)
                            nc.vector.bn_aggr(mv[:, s, :], stats[:, s, :]).then_inc(st, 1)
                        dve.wait_ge(st, 2 * NS)
                        nc.vector.tensor_scalar(rstd[:, :], mv[:, :, 1], EPS, None, ALU.add).then_inc(var_ok, 1)
                        dve.wait_ge(rstd_ok, 1)
                        for s in range(NS):
                            nc.vector.tensor_scalar(U[:, s, :], X[:, s, :], mv[:, s, 0:1], rstd[:, s:s + 1],
                                                    ALU.subtract, ALU.mult).then_inc(done, 1)
                stack.pop()
                end_phase([x_in, var_ok, rstd_ok, st, done])

        def ffn_phase():
            with ExitStack() as scope:
                stack.append(scope)
                HT = sb("HT", [P, NB, T + 1])
                HT2 = sb("HT2", [P, NB, T + 1])
                RA = sb("RA", [P, 2, 2, NH, DH])
                RB = sb("RB", [P, 2, NH, DH])
                SQ = sb("SQ", [P, 2 * NH, DH])
                SS = sb("SS", [P, 2 * NH])
                RN = sb("RN", [P, 2, 2 * NH])
                QZ = sb("QZ", [P, NH, P])
                KT = sb("KT", [P, CH, NB, W + T])
                VB = sb("VB", [P, NB, NT, NH, DH + 1])
                VA = sb("VA", [P, NB, NT, NH, DH + 1])
                PR = sb("PR", [P, NH, P])
                PT = sb("PT", [P, NH, P])
                NMX = sb("NMX", [P, NH])
                RS = sb("RS", [P, NH])
                ON = sb("ON", [P, NH, DH])
                OT = sb("OT", [P, CH, P])
                U2 = sb("U2", [P, 2, P])
                U2B = sb("U2B", [P, 2, P])
                DT = sb("DT", [P, P]); SQ2 = sb("SQ2", [P, P]); DG_ = sb("DG_", [P, P]); HN = sb("HN", [P, P])
                VE = sb("VE", [P, 1]); RV = sb("RV", [P, 1])
                GL = sb("GL", [HC, 3, P]); GLU = sb("GLU", [HC, 3, P])

                S = {n: sem(n) for n in (
                    "preset uT_in u2T_in ht_ok ht2_ok q_in k_in v_in kmul qmul ksq sq_ok ss_ok qsum_ok ksum_ok rn_ok qrot_ok krot_ok "
                    "qT_in kT_in qz_ok kt_ok s0_in s1_in nmx0_ok nmx1_ok p0_ok p1_ok pt0_in pt1_in pt0_ok pt1_ok vb_ok va_ok o_in on_ok "
                    "ot_in ot_ok wo_in u2_ok u2b_ok mean_in dt_ok sq2_ok var_in ve_ok rv_ok dg_ok bc_in hn_ok "
                    "w1a_in w1g_in gl_ok glu_ok w2_in u3_ok dch").split()}
                NU = DEPTH * NS
                STEPS = range(NU + 6)
                B_UT, B_U2T, B_MEAN, B_VAR, B_BC = 5, 2, 2, 3, 4
                B_QKV, B_TURN = (7, 1, 6), (7, 1)
                B_S, B_PT, B_PV, B_OT, B_WO = (1, 5), (3, 5), (0, 4), 4, 2
                B_W1G, B_W1A, B_W2 = 3, 6, 0

                def unit(n):
                    s = n % NS
                    return n // NS, s // NT, s % NT, s

                def live(n):
                    return 0 <= n < NU

                with nc.Block() as block:
                    @block.tensor
                    def _(pe):
                        readers = [None] * 8

                        def claim(k, name, count):
                            if readers[k]:
                                pe.wait_ge(*readers[k])
                            readers[k] = (S[name], count)

                        def turn(u, g):
                            pe.wait_ge(S[("qrot_ok", "krot_ok")[g]], u + 1)
                            claim(B_TURN[g], ("qz_ok", "kt_ok")[g], u + 1)
                            for j in range(CH):
                                last = pe.transpose(BK[B_TURN[g]][:, j * P:(j + 1) * P],
                                                    RA[:, u % 2, g, 2 * j:2 * j + 2, :], ident)
                            last.then_inc(S[("qT_in", "kT_in")[g]], 1)

                        def project(u, k):
                            l, bb, t, s = unit(u)
                            return nc.tensor.matmul(BK[B_QKV[k]][:, :], HT[:, bb, t * P:(t + 1) * P],
                                                    wqkv_s[:, l, k * 512:(k + 1) * 512], start=True, stop=True)

                        def scores(u, g):
                            l, bb, t, s = unit(u)
                            nc.tensor.matmul(BK[B_S[g]][:, :].rearrange("p (a b) -> p a b", a=4), identb[:, :],
                                             maskb[:, 1 if t == 0 else 0, :].unsqueeze(1).to_broadcast([P, 4, P]),
                                             start=True, stop=False, skip_group_check=True)
                            for h in range(4 * g, 4 * g + 4):
                                for w in range(2):
                                    k0 = (2 * t + w) * W
                                    last = nc.tensor.matmul(
                                        BK[B_S[g]][w * W:(w + 1) * W, (h % 4) * P:(h % 4 + 1) * P],
                                        QZ[:, h, w * W:(w + 1) * W], KT[:, h // 2, bb, k0:k0 + 2 * W],
                                        start=False, stop=True, skip_group_check=True)
                            return last

                        def hidden(l, g, k):
                            for j in range(3):
                                o = g * HID + j * HC
                                last = nc.tensor.matmul(BK[k][0:HCS[j], j * P:(j + 1) * P],
                                                        w1_s[:, l, o:o + HCS[j]], HN[:, :], start=True, stop=True)
                            return last

                        pe.wait_ge(S["preset"], 6)
                        for n in STEPS:
                            u = n - 3
                            if live(u):
                                pe.wait_ge(S["p1_ok"], u + 1)
                                claim(B_PT[1], "pt1_ok", u + 1)
                                for h in range(4):
                                    last = pe.transpose(BK[B_PT[1]][:, h * P:(h + 1) * P], PR[:, 4 + h, :], ident)
                                last.then_inc(S["pt1_in"], 1)
                            u = n - 5
                            if live(u):
                                pe.wait_ge(S["dg_ok"], u + 1)
                                claim(B_BC, "hn_ok", u + 1)
                                nc.tensor.matmul(BK[B_BC][:, 0:P], ones[:, :], DG_[:, :],
                                                 start=True, stop=True).then_inc(S["bc_in"], 1)
                            u = n - 4
                            if live(u):
                                pe.wait_ge(S["u2_ok"], u + 1)
                                claim(B_U2T, "ht2_ok", u + 1)
                                pe.transpose(BK[B_U2T][:, 0:P], U2[:, u % 2, :], ident).then_inc(S["u2T_in"], 1)
                            u = n - 2
                            if live(u):
                                turn(u, 1)
                            u = n - 2
                            if live(u):
                                turn(u, 0)
                            u = n - 3
                            if live(u):
                                l, bb, t, s = unit(u)
                                pe.wait_ge(S["pt0_ok"], u + 1)
                                pe.wait_ge(S["pt1_ok"], u + 1)
                                pe.wait_ge(S["va_ok"], u + 1)
                                claim(B_PV[0], "on_ok", 2 * u + 1)
                                claim(B_PV[1], "on_ok", 2 * u + 2)
                                for h in range(NH):
                                    for w in range(2):
                                        o = (h % 4) * (DH + 1)
                                        last = nc.tensor.matmul(BK[B_PV[h // 4]][w * W:(w + 1) * W, o:o + DH + 1],
                                                                PT[:, h, w * W:(w + 1) * W], (VA, VB)[w][:, bb, t, h, :],
                                                                start=True, stop=True)
                                last.then_inc(S["o_in"], 1)
                            u = n - 5
                            if live(u):
                                pe.wait_ge(S["hn_ok"], u + 1)
                                claim(B_W1G, "gl_ok", u + 1)
                                hidden(unit(u)[0], 1, B_W1G).then_inc(S["w1g_in"], 1)
                            u = n
                            if live(u):
                                if u >= NS:
                                    pe.wait_ge(S["u3_ok"], u - NS + 1)
                                claim(B_UT, "ht_ok", u + 1)
                                pe.transpose(BK[B_UT][:, 0:P], U[:, unit(u)[3], :], ident).then_inc(S["uT_in"], 1)
                            u = n - 2
                            if live(u):
                                pe.wait_ge(S["qz_ok"], u + 1)
                                pe.wait_ge(S["kt_ok"], u + 1)
                                claim(B_S[0], "p0_ok", u + 1)
                                scores(u, 0).then_inc(S["s0_in"], 1)
                            u = n - 4
                            if live(u):
                                l, bb, t, s = unit(u)
                                pe.wait_ge(S["ht2_ok"], u + 1)
                                claim(B_MEAN, "dt_ok", u + 1)
                                nc.tensor.matmul(BK[B_MEAN][:, 0:P], meanw[:, :], HT2[:, bb, t * P:(t + 1) * P],
                                                 start=True, stop=True).then_inc(S["mean_in"], 1)
                            u = n - 5
                            if live(u):
                                pe.wait_ge(S["hn_ok"], u + 1)
                                claim(B_W1A, "glu_ok", u + 1)
                                hidden(unit(u)[0], 0, B_W1A).then_inc(S["w1a_in"], 1)
                            u = n - 3
                            if live(u):
                                pe.wait_ge(S["on_ok"], 2 * u + 2)
                                claim(B_OT, "ot_ok", u + 1)
                                for j in range(CH):
                                    last = pe.transpose(BK[B_OT][:, j * P:(j + 1) * P], ON[:, 2 * j:2 * j + 2, :], ident)
                                last.then_inc(S["ot_in"], 1)
                            u = n
                            if live(u):
                                pe.wait_ge(S["ht_ok"], u + 1)
                                claim(B_QKV[0], "sq_ok", u + 1)
                                project(u, 0).then_inc(S["q_in"], 1)
                            u = n - 2
                            if live(u):
                                claim(B_S[1], "p1_ok", u + 1)
                                scores(u, 1).then_inc(S["s1_in"], 1)
                            u = n
                            if live(u):
                                pe.wait_ge(S["ht_ok"], u + 1)
                                claim(B_QKV[1], "kmul", u + 1)
                                project(u, 1).then_inc(S["k_in"], 1)
                            u = n - 4
                            if live(u):
                                pe.wait_ge(S["sq2_ok"], u + 1)
                                claim(B_VAR, "ve_ok", u + 1)
                                nc.tensor.matmul(BK[B_VAR][:, 0:1], SQ2[:, :], meanw[:, 0:1],
                                                 start=True, stop=True).then_inc(S["var_in"], 1)
                            u = n - 3
                            if live(u):
                                l = unit(u)[0]
                                pe.wait_ge(S["ot_ok"], u + 1)
                                claim(B_WO, "u2_ok", u + 1)
                                for j in range(CH):
                                    last = nc.tensor.matmul(BK[B_WO][:, 0:P], OT[:, j, :], wo_s[:, l, j, :],
                                                            start=(j == 0), stop=(j == CH - 1))
                                last.then_inc(S["wo_in"], 1)
                            u = n
                            if live(u):
                                pe.wait_ge(S["ht_ok"], u + 1)
                                claim(B_QKV[2], "vb_ok", u + 1)
                                project(u, 2).then_inc(S["v_in"], 1)
                            u = n - 5
                            if live(u):
                                l = unit(u)[0]
                                pe.wait_ge(S["glu_ok"], u + 1)
                                claim(B_W2, "u3_ok", u + 1)
                                for j in range(3):
                                    last = nc.tensor.matmul(BK[B_W2][:, 0:P], GLU[0:HCS[j], j, :], w2_s[0:HCS[j], l, j, :],
                                                            start=(j == 0), stop=(j == 2))
                                last.then_inc(S["w2_in"], 1)
                            u = n - 2
                            if live(u):
                                pe.wait_ge(S["p0_ok"], u + 1)
                                claim(B_PT[0], "pt0_ok", u + 1)
                                for h in range(4):
                                    last = pe.transpose(BK[B_PT[0]][:, h * P:(h + 1) * P], PR[:, 0 + h, :], ident)
                                last.then_inc(S["pt0_in"], 1)

                    @block.scalar
                    def _(act):
                        def softmax_exp(u, g):
                            act.wait_ge(S[("nmx0_ok", "nmx1_ok")[g]], u + 1)
                            if u >= 1:
                                act.wait_ge(S[("pt0_in", "pt1_in")[g]], u)
                            for h in range(4):
                                last = nc.scalar.activation(PR[:, 4 * g + h, :], BK[B_S[g]][:, h * P:(h + 1) * P],
                                                            ACT.Exp, bias=NMX[:, 4 * g + h:4 * g + h + 1], scale=8.0)
                            return last

                        act.wait_ge(S["preset"], 6)
                        for n in STEPS:
                            u = n - 4
                            if live(u):
                                act.wait_ge(S["ot_in"], u + 1)
                                if u >= 1:
                                    act.wait_ge(S["wo_in"], u)
                                nc.scalar.activation(OT[:, :, :], BK[B_OT][:, :].rearrange("p (c q) -> p c q", c=CH),
                                                     ACT.Copy).then_inc(S["ot_ok"], 1)
                            u = n - 1
                            if live(u):
                                act.wait_ge(S["k_in"], u + 1)
                                if u >= 1:
                                    act.wait_ge(S["ss_ok"], u)
                                nc.scalar.activation(SQ[:, NH:2 * NH, :], BK[B_QKV[1]][:, :].rearrange("p (h d) -> p h d", h=NH),
                                                     ACT.Square).then_inc(S["ksq"], 1)
                            u = n - 3
                            if live(u):
                                softmax_exp(u, 1).then_inc(S["p1_ok"], 1)
                            u = n - 1
                            if live(u):
                                act.wait_ge(S["qmul"], u + 1)
                                if u >= 1:
                                    act.wait_ge(S["ss_ok"], u)
                                nc.scalar.activation(SQ[:, 0:NH, :], BK[B_QKV[0]][:, :].rearrange("p (h d) -> p h d", h=NH),
                                                     ACT.Square).then_inc(S["sq_ok"], 1)
                            u = n - 3
                            if live(u):
                                act.wait_ge(S["pt1_in"], u + 1)
                                if u >= 1:
                                    act.wait_ge(S["o_in"], u)
                                nc.scalar.activation(PT[:, 4:8, :], BK[B_PT[1]][:, :].rearrange("p (h q) -> p h q", h=4),
                                                     ACT.Copy).then_inc(S["pt1_ok"], 1)
                            u = n - 1
                            if live(u):
                                l, bb, t, s = unit(u)
                                act.wait_ge(S["v_in"], u + 1)
                                nc.scalar.activation(VB[:, bb, t, :, 0:DH], BK[B_QKV[2]][:, :].rearrange("p (h d) -> p h d", h=NH),
                                                     ACT.Copy).then_inc(S["vb_ok"], 1)
                            u = n - 2
                            if live(u):
                                act.wait_ge(S["qT_in"], u + 1)
                                if u >= 1:
                                    act.wait_ge(S["s1_in"], u)
                                for hf in range(2):
                                    src = BK[B_TURN[0]][hf * W:(hf + 1) * W, :].rearrange("p (c q) -> p c q", c=CH)
                                    last = nc.scalar.activation(QZ[hf * W:(hf + 1) * W, hf::2, :], src, ACT.Copy)
                                last.then_inc(S["qz_ok"], 1)
                            u = n - 5
                            if live(u):
                                l = unit(u)[0]
                                act.wait_ge(S["w1g_in"], u + 1)
                                if u >= 1:
                                    act.wait_ge(S["glu_ok"], u)
                                for j in range(3):
                                    last = nc.scalar.activation(GL[0:HCS[j], j, :], BK[B_W1G][0:HCS[j], j * P:(j + 1) * P],
                                                                ACT.Gelu, bias=b1_s[0:HCS[j], l, 1, j:j + 1])
                                last.then_inc(S["gl_ok"], 1)
                            u = n - 2
                            if live(u):
                                softmax_exp(u, 0).then_inc(S["p0_ok"], 1)

                    @block.vector
                    def _(dve):
                        chain = [0]

                        def link(ins):
                            chain[0] += 1
                            ins.then_inc(S["dch"], 1)
                            dve.wait_ge(S["dch"], chain[0])

                        def rowmax(u, g):
                            dve.wait_ge(S[("s0_in", "s1_in")[g]], u + 1)
                            if u >= 1:
                                dve.wait_ge(S[("p0_ok", "p1_ok")[g]], u)
                            c = NMX[:, 4 * g:4 * g + 4]
                            link(nc.vector.tensor_reduce(c, BK[B_S[g]][:, :].rearrange("p (h q) -> p h q", h=4),
                                                         AX_X, ALU.max))
                            nc.vector.tensor_scalar(c, c, -8.0, None, ALU.mult).then_inc(S[("nmx0_ok", "nmx1_ok")[g]], 1)

                        def rotary(u, g):
                            l, bb, t, s = unit(u)
                            dve.wait_ge(S[("q_in", "k_in")[g]], u + 1)
                            if g == 1:
                                dve.wait_ge(S["ksq"], u + 1)
                            if u >= 1:
                                dve.wait_ge(S[("qsum_ok", "ksum_ok")[g]], u)
                            if u >= 2:
                                dve.wait_ge(S[("qT_in", "kT_in")[g]], u - 1)
                            bank = BK[B_QKV[g]]
                            src = bank[:, :].rearrange("p (h d) -> p h d", h=NH)
                            rot = bank[:, :].rearrange("p (h z d) -> p h z d", h=NH, z=2)[:, :, ::-1, :]
                            nc.vector.tensor_tensor(RA[:, u % 2, g, :, :], src,
                                                    ropet[:, l, t, 2 * g, :].unsqueeze(1).to_broadcast([P, NH, DH]),
                                                    ALU.mult)
                            tab = ropet[:, l, t, 2 * g + 1, :].rearrange("p (z d) -> p z d", z=2)
                            nc.vector.tensor_tensor(
                                RB[:, g, :, :].rearrange("p h (z d) -> p h z d", z=2), rot,
                                tab.unsqueeze(1).to_broadcast([P, NH, 2, DH // 2]),
                                ALU.mult).then_inc(S[("qmul", "kmul")[g]], 1)

                        def shifted(m, src, dst, inn, okk):
                            l, bb, t, s = unit(m)
                            dve.wait_ge(S[inn], m + 1)
                            nc.vector.tensor_copy(dst[0:W, bb, t * P:(t + 1) * P], BK[src][0:W, 0:P])
                            nc.vector.tensor_copy(dst[W:P, bb, t * P + 1:(t + 1) * P + 1],
                                                  BK[src][W:P, 0:P]).then_inc(S[okk], 1)

                        nc.vector.memset(HT[W:P, :, 0:1], 0.0).then_inc(S["preset"], 1)
                        nc.vector.memset(HT2[W:P, :, 0:1], 0.0).then_inc(S["preset"], 1)
                        nc.vector.memset(VB[:, :, :, :, DH:DH + 1], 1.0).then_inc(S["preset"], 1)
                        nc.vector.memset(KT[:, :, :, 0:W], 0.0).then_inc(S["preset"], 1)
                        nc.vector.memset(VA[0:W, :, 0, :, :], 0.0)
                        nc.vector.memset(QZ[0:W, 1::2, :], 0.0).then_inc(S["preset"], 1)
                        nc.vector.memset(QZ[W:P, 0::2, :], 0.0).then_inc(S["preset"], 1)
                        dve.wait_ge(S["preset"], 6)
                        for n in STEPS:
                            u = n - 5
                            if live(u):
                                dve.wait_ge(S["rv_ok"], u + 1)
                                if u >= 1:
                                    dve.wait_ge(S["bc_in"], u)
                                nc.vector.tensor_scalar(DG_[:, :], ident, RV[:, 0:1], None, ALU.mult).then_inc(S["dg_ok"], 1)
                            u = n - 1
                            if live(u):
                                rotary(u, 1)
                            u = n - 6
                            if live(u):
                                l, bb, t, s = unit(u)
                                dve.wait_ge(S["w2_in"], u + 1)
                                dve.wait_ge(S["u2b_ok"], u + 1)
                                nc.vector.tensor_tensor(U[:, s, :], BK[B_W2][:, 0:P], U2B[:, u % 2, :],
                                                        ALU.add).then_inc(S["u3_ok"], 1)
                                if l == DEPTH - 1:
                                    dve.wait_ge(S["u3_ok"], u + 1)
                                    nc.vector.scalar_tensor_tensor(out=X[:, s, :], in0=U[:, s, :], scalar=0.5,
                                                                   in1=X[:, s, :], op0=ALU.mult, op1=ALU.add)
                            u = n - 3
                            if live(u):
                                dve.wait_ge(S["pt0_in"], u + 1)
                                if u >= 1:
                                    dve.wait_ge(S["o_in"], u)
                                nc.vector.tensor_copy(PT[:, 0:4, :], BK[B_PT[0]][:, :].rearrange("p (h q) -> p h q", h=4)).then_inc(S["pt0_ok"], 1)
                            u = n - 5
                            if live(u):
                                dve.wait_ge(S["bc_in"], u + 1)
                                if u >= 1:
                                    dve.wait_ge(S["w1g_in"], u)
                                    dve.wait_ge(S["w1a_in"], u)
                                nc.vector.tensor_tensor(HN[:, :], BK[B_BC][:, 0:P], DT[:, :], ALU.mult).then_inc(S["hn_ok"], 1)
                            u = n - 4
                            if live(u):
                                shifted(u, B_U2T, HT2, "u2T_in", "ht2_ok")
                            u = n - 2
                            if live(u):
                                l, bb, t, s = unit(u)
                                dve.wait_ge(S["kT_in"], u + 1)
                                nc.vector.tensor_copy(KT[:, :, bb, W + t * P:W + (t + 1) * P],
                                                      BK[B_TURN[1]][:, :].rearrange("p (c q) -> p c q", c=CH)).then_inc(S["kt_ok"], 1)
                            u = n - 1
                            if live(u):
                                dve.wait_ge(S["sq_ok"], u + 1)
                                dve.wait_ge(S["ksq"], u + 1)
                                if u >= 1:
                                    dve.wait_ge(S["rn_ok"], u)
                                link(nc.vector.tensor_reduce(SS[:, :], SQ[:, :, :], AX_X, ALU.add))
                                nc.vector.tensor_scalar(SS[:, :], SS[:, :], 1e-24, None, ALU.max).then_inc(S["ss_ok"], 1)
                            u = n - 3
                            if live(u):
                                dve.wait_ge(S["o_in"], u + 1)
                                if u >= 1:
                                    dve.wait_ge(S["ot_in"], u)
                                for g in range(2):
                                    O = BK[B_PV[g]][:, 0:4 * (DH + 1)].rearrange("p (h d) -> p h d", h=4)
                                    link(nc.vector.reciprocal(RS[:, 4 * g:4 * g + 4], O[:, :, DH]))
                                    nc.vector.tensor_tensor(ON[:, 4 * g:4 * g + 4, :], O[:, :, 0:DH],
                                                            RS[:, 4 * g:4 * g + 4].unsqueeze(2).to_broadcast([P, 4, DH]),
                                                            ALU.mult).then_inc(S["on_ok"], 1)
                            u = n
                            if live(u):
                                shifted(u, B_UT, HT, "uT_in", "ht_ok")
                            u = n - 2
                            if live(u):
                                rowmax(u, 0)
                            u = n - 4
                            if live(u):
                                l, bb, t, s = unit(u)
                                dve.wait_ge(S["mean_in"], u + 1)
                                nc.vector.scalar_tensor_tensor(
                                    out=DT[:, :], in0=BK[B_MEAN][:, 0:P], scalar=-1.0, in1=HT2[:, bb, t * P:(t + 1) * P],
                                    op0=ALU.mult, op1=ALU.add).then_inc(S["dt_ok"], 1)
                                dve.wait_ge(S["dt_ok"], u + 1)
                                if u >= 1:
                                    dve.wait_ge(S["var_in"], u)
                                nc.vector.tensor_tensor(SQ2[:, :], DT[:, :], DT[:, :], ALU.mult).then_inc(S["sq2_ok"], 1)
                            u = n - 5
                            if live(u):
                                l = unit(u)[0]
                                dve.wait_ge(S["w1a_in"], u + 1)
                                dve.wait_ge(S["gl_ok"], u + 1)
                                if u >= 1:
                                    dve.wait_ge(S["w2_in"], u)
                                for j in range(3):
                                    h_ = HCS[j]
                                    last = nc.vector.scalar_tensor_tensor(
                                        out=GLU[0:h_, j, :], in0=BK[B_W1A][0:h_, j * P:(j + 1) * P],
                                        scalar=b1_s[0:h_, l, 0, j:j + 1], in1=GL[0:h_, j, :], op0=ALU.add, op1=ALU.mult)
                                last.then_inc(S["glu_ok"], 1)
                            u = n
                            if live(u):
                                rotary(u, 0)
                            u = n - 2
                            if live(u):
                                rowmax(u, 1)
                            u = n - 4
                            if live(u):
                                dve.wait_ge(S["var_in"], u + 1)
                                if u >= 1:
                                    dve.wait_ge(S["rv_ok"], u)
                                nc.vector.tensor_scalar(VE[:, :], BK[B_VAR][:, 0:1], EPS, None, ALU.add).then_inc(S["ve_ok"], 1)
                            u = n - 2
                            if live(u):
                                l, bb, t, s = unit(u)
                                dve.wait_ge(S["vb_ok"], u + 1)
                                if t < NT - 1:
                                    nc.vector.tensor_copy(VA[0:W, bb, t + 1, :, :], VB[W:P, bb, t, :, :])
                                nc.vector.tensor_copy(VA[W:P, bb, t, :, :], VB[0:W, bb, t, :, :]).then_inc(S["va_ok"], 1)
                            u = n - 3
                            if live(u):
                                s = unit(u)[3]
                                dve.wait_ge(S["wo_in"], u + 1)
                                if u >= 2:
                                    dve.wait_ge(S["u2T_in"], u - 1)
                                    dve.wait_ge(S["u2b_ok"], u - 1)
                                nc.vector.tensor_tensor(U2[:, u % 2, :], BK[B_WO][:, 0:P], U[:, s, :], ALU.add).then_inc(S["u2_ok"], 1)

                    @block.gpsimd
                    def _(pool):
                        for n in STEPS:
                            u = n - 6
                            if live(u):
                                l = unit(u)[0]
                                pool.wait_ge(S["u2_ok"], u + 1)
                                if u >= 2:
                                    pool.wait_ge(S["u3_ok"], u - 1)
                                nc.gpsimd.tensor_tensor(U2B[:, u % 2, :], U2[:, u % 2, :], b2_s[:, l, :], ALU.add).then_inc(S["u2b_ok"], 1)
                            u = n - 5
                            if live(u):
                                pool.wait_ge(S["ve_ok"], u + 1)
                                if u >= 1:
                                    pool.wait_ge(S["dg_ok"], u)
                                nc.gpsimd.tensor_tensor(RV[:, :], VE[:, :], mhalf[:, 0:1], ALU.pow).then_inc(S["rv_ok"], 1)
                            u = n - 1
                            if live(u):
                                pool.wait_ge(S["qmul"], u + 1)
                                nc.gpsimd.tensor_tensor(RA[:, u % 2, 0, :, :], RA[:, u % 2, 0, :, :], RB[:, 0, :, :],
                                                        ALU.add).then_inc(S["qsum_ok"], 1)
                            u = n - 1
                            if live(u):
                                pool.wait_ge(S["kmul"], u + 1)
                                nc.gpsimd.tensor_tensor(RA[:, u % 2, 1, :, :], RA[:, u % 2, 1, :, :], RB[:, 1, :, :],
                                                        ALU.add).then_inc(S["ksum_ok"], 1)
                            u = n - 1
                            if live(u):
                                pool.wait_ge(S["ss_ok"], u + 1)
                                nc.gpsimd.tensor_tensor(RN[:, u % 2, :], SS[:, :], mhalf[:, 0:2 * NH], ALU.pow).then_inc(S["rn_ok"], 1)
                            u = n - 1
                            if live(u):
                                pool.wait_ge(S["rn_ok"], u + 1)
                                pool.wait_ge(S["ksum_ok"], u + 1)
                                nc.gpsimd.tensor_tensor(RA[:, u % 2, 1, :, :], RA[:, u % 2, 1, :, :],
                                                        RN[:, u % 2, NH:2 * NH].unsqueeze(2).to_broadcast([P, NH, DH]),
                                                        ALU.mult).then_inc(S["krot_ok"], 1)
                            u = n - 1
                            if live(u):
                                pool.wait_ge(S["rn_ok"], u + 1)
                                pool.wait_ge(S["qsum_ok"], u + 1)
                                nc.gpsimd.tensor_tensor(RA[:, u % 2, 0, :, :], RA[:, u % 2, 0, :, :],
                                                        RN[:, u % 2, 0:NH].unsqueeze(2).to_broadcast([P, NH, DH]),
                                                        ALU.mult).then_inc(S["qrot_ok"], 1)
                stack.pop()
                end_phase(list(S.values()))

        def mla_phase():
            with ExitStack() as scope:
                stack.append(scope)
                XT = sb("XT", [P, T]); QT = sb("QT", [P, T]); KL = sb("KL", [P, T])
                QZL = sb("QZL", [P, NG, T])
                VL = sb("VL", [P, NT, NG, 32])
                PL = sb("PL", [P, 3, T])
                PTL = sb("PTL", [P, 2, LG, NT, T])
                OTL = sb("OTL", [P, T])
                RL = sb("RL", [P, NT, LG])
                Y = sb("Y", [P, NT, LG, DG])
                NM = sb("NM", [P, 4])
                S = {n: sem(n) for n in (
                    "preset xt_in xt_ok q_in k_in v_in qt_ok kl_ok vl_ok qz_ok s_in nm_ok p_ok pt_in pt_ok o_in "
                    "ot_ok y_in y_ok pv_done dch").split()}
                NM_UNITS = NG * NT
                SCALE = float(DG) ** -0.5
                GROUPS = NG // LG
                PER = NT * LG

                def munit(m):
                    g, r = divmod(m, PER)
                    i, hh = divmod(r, LG)
                    return g, i, hh, g * LG + hh

                def evac(eng, ops, S, bb, M0, k):
                    g, i, hh, h = munit(k)
                    kk = M0 + k
                    eng.wait_ge(S["pt_in"], kk + 1)
                    if kk >= 2 * PER:
                        eng.wait_ge(S["o_in"], kk // PER - 1)
                    if kk >= 1:
                        eng.wait_ge(S["pt_ok"], kk)
                    dst = PTL[:, kk // PER % 2, hh, 0:i + 1, i * P:(i + 1) * P]
                    src = BK[4 + kk % 2][:, 0:(i + 1) * P].rearrange("p (j q) -> p j q", q=P)
                    if k % 2:
                        ops.activation(dst, src, ACT.Copy).then_inc(S["pt_ok"], 1)
                    else:
                        ops.tensor_copy(dst, src).then_inc(S["pt_ok"], 1)

                with nc.Block() as block:
                    @block.tensor
                    def _(pe):
                        pe.wait_ge(S["preset"], 1)
                        for bb in range(NB):
                            M0 = bb * NM_UNITS
                            G0 = bb * GROUPS
                            if bb:
                                pe.wait_ge(S["y_ok"], G0)
                            for t in range(NT):
                                last = pe.transpose(BK[7][:, t * P:(t + 1) * P], U[:, bb * NT + t, :], ident)
                            last.then_inc(S["xt_in"], 1)
                            pe.wait_ge(S["xt_ok"], bb + 1)
                            if bb:
                                pe.wait_ge(S["p_ok"], M0)
                            nc.tensor.matmul(BK[0][:, :], Wq_s[:, :], XT[:, :], start=True, stop=True).then_inc(S["q_in"], 1)
                            nc.tensor.matmul(BK[1][:, :], Wk_s[:, :], XT[:, :], start=True, stop=True).then_inc(S["k_in"], 1)
                            for t in range(NT):
                                last = nc.tensor.matmul(BK[2][:, t * P:(t + 1) * P], XT[:, t * P:(t + 1) * P], Wv_s[:, :],
                                                        start=True, stop=True)
                            last.then_inc(S["v_in"], 1)
                            pe.wait_ge(S["qt_ok"], bb + 1)
                            pe.wait_ge(S["kl_ok"], bb + 1)
                            pe.wait_ge(S["vl_ok"], bb + 1)
                            for m in range(NM_UNITS + 8):
                                if m < NM_UNITS:
                                    g, i, hh, h = munit(m)
                                    mm_ = M0 + m
                                    if i == 0:
                                        pe.wait_ge(S["qz_ok"], bb * NG + h + 1)
                                    if m >= 4:
                                        pe.wait_ge(S["p_ok"], mm_ - 3)
                                    bk = BK[mm_ % 4]
                                    N = (i + 1) * P
                                    nc.tensor.matmul(bk[:, 0:N], QZL[:, h, i * P:(i + 1) * P], KL[:, 0:N],
                                                     start=True, stop=False, skip_group_check=True)
                                    nc.tensor.matmul(bk[:, i * P:N], identb[:, :], maskb[:, 2, :],
                                                     start=False, stop=True, skip_group_check=True).then_inc(S["s_in"], 1)
                                if 2 <= m < NM_UNITS + 2:
                                    k = m - 2
                                    g, i, hh, h = munit(k)
                                    kk = M0 + k
                                    pe.wait_ge(S["p_ok"], kk + 1)
                                    if kk >= 2:
                                        pe.wait_ge(S["pt_ok"], kk - 1)
                                    for j in range(i + 1):
                                        last = pe.transpose(BK[4 + kk % 2][:, j * P:(j + 1) * P],
                                                            PL[:, kk % 3, j * P:(j + 1) * P], ident)
                                    last.then_inc(S["pt_in"], 1)
                                k = m - 4
                                if k >= 0 and k % PER == PER - 1:
                                    g = k // PER
                                    gg = G0 + g
                                    pe.wait_ge(S["pt_ok"], M0 + k + 1)
                                    if gg >= 1:
                                        pe.wait_ge(S["ot_ok"], gg)
                                    for j in range(NT):
                                        for q in range(LG):
                                            last = nc.tensor.matmul(BK[6][32 * q:32 * q + 32, j * P:T],
                                                                    VL[:, j, g * LG + q, :], PTL[:, gg % 2, q, j, j * P:T],
                                                                    start=(j == 0), stop=(j == NT - 1),
                                                                    skip_group_check=True)
                                    last.then_inc(S["o_in"], 1)
                                k = m - 6
                                if k >= 0 and k % PER == PER - 1:
                                    gg = G0 + k // PER
                                    pe.wait_ge(S["ot_ok"], gg + 1)
                                    if gg >= 1:
                                        pe.wait_ge(S["y_ok"], gg)
                                    for t in range(NT):
                                        last = pe.transpose(BK[7][:, t * P:(t + 1) * P], OTL[:, t * P:(t + 1) * P], ident)
                                    last.then_inc(S["y_in"], 1)

                    @block.scalar
                    def _(act):
                        act.wait_ge(S["preset"], 1)
                        for bb in range(NB):
                            M0, G0 = bb * NM_UNITS, bb * GROUPS
                            act.wait_ge(S["v_in"], bb + 1)
                            nc.scalar.activation(VL[:, :, :, 0:DG], BK[2][:, :].rearrange("p (t h d) -> p t h d", t=NT, h=NG),
                                                 ACT.Copy).then_inc(S["vl_ok"], 1)
                            for m in range(NM_UNITS + 8):
                                if m < NM_UNITS:
                                    g, i, hh, h = munit(m)
                                    mm_ = M0 + m
                                    N = (i + 1) * P
                                    act.wait_ge(S["nm_ok"], mm_ + 1)
                                    if mm_ >= 3:
                                        act.wait_ge(S["pt_in"], mm_ - 2)
                                    nc.scalar.activation(PL[:, mm_ % 3, 0:N], BK[mm_ % 4][:, 0:N], ACT.Exp,
                                                         bias=NM[:, mm_ % 4:mm_ % 4 + 1], scale=SCALE).then_inc(S["p_ok"], 1)
                                k = m - 3
                                if 0 <= k < NM_UNITS and k % 2 == 1:
                                    evac(act, nc.scalar, S, bb, M0, k)

                    @block.vector
                    def _(dve):
                        chain = [0]

                        def link(ins):
                            chain[0] += 1
                            ins.then_inc(S["dch"], 1)
                            dve.wait_ge(S["dch"], chain[0])

                        link(nc.vector.memset(VL[:, :, :, :], 0.0))
                        nc.vector.memset(VL[:, :, :, DG:DG + 1], 1.0).then_inc(S["preset"], 1)
                        dve.wait_ge(S["preset"], 1)
                        for bb in range(NB):
                            M0, G0 = bb * NM_UNITS, bb * GROUPS
                            dve.wait_ge(S["xt_in"], bb + 1)
                            nc.vector.tensor_copy(XT[:, :], BK[7][:, :]).then_inc(S["xt_ok"], 1)
                            dve.wait_ge(S["q_in"], bb + 1)
                            nc.vector.tensor_copy(QT[:, :], BK[0][:, :]).then_inc(S["qt_ok"], 1)
                            dve.wait_ge(S["k_in"], bb + 1)
                            nc.vector.tensor_copy(KL[:, :], BK[1][:, :]).then_inc(S["kl_ok"], 1)
                            dve.wait_ge(S["qt_ok"], bb + 1)
                            for h in range(NG):
                                nc.vector.tensor_scalar(QZL[:, h, :], QT[:, :], headsel[:, h:h + 1], None,
                                                        ALU.mult).then_inc(S["qz_ok"], 1)
                            for m in range(NM_UNITS + 8):
                                if m < NM_UNITS:
                                    g, i, hh, h = munit(m)
                                    mm_ = M0 + m
                                    N = (i + 1) * P
                                    dve.wait_ge(S["s_in"], mm_ + 1)
                                    if mm_ >= 4:
                                        dve.wait_ge(S["p_ok"], mm_ - 3)
                                    c = NM[:, mm_ % 4:mm_ % 4 + 1]
                                    link(nc.vector.tensor_reduce(c, BK[mm_ % 4][:, 0:N], AX_X, ALU.max))
                                    nc.vector.tensor_scalar(c, c, -SCALE, None, ALU.mult).then_inc(S["nm_ok"], 1)
                                k = m - 3
                                if 0 <= k < NM_UNITS and k % 2 == 0:
                                    evac(dve, nc.vector, S, bb, M0, k)
                                k = m - 5
                                if k >= 0 and k % PER == PER - 1:
                                    gg = G0 + k // PER
                                    dve.wait_ge(S["o_in"], gg + 1)
                                    if gg >= 1:
                                        dve.wait_ge(S["y_in"], gg)
                                    nc.vector.tensor_copy(OTL[:, :], BK[6][:, :]).then_inc(S["ot_ok"], 1)
                                k = m - 7
                                if k >= 0 and k % PER == PER - 1:
                                    g = k // PER
                                    gg = G0 + g
                                    dve.wait_ge(S["y_in"], gg + 1)
                                    O = BK[7][:, :].rearrange("p (t h d) -> p t h d", t=NT, h=LG)
                                    link(nc.vector.reciprocal(RL[:, :, :], O[:, :, :, DG]))
                                    nc.vector.tensor_tensor(Y[:, :, :, :], O[:, :, :, 0:DG],
                                                                 RL[:, :, :].unsqueeze(3).to_broadcast([P, NT, LG, DG]),
                                                                 ALU.mult).then_inc(S["y_ok"], 1)
                                    dve.wait_ge(S["y_ok"], gg + 1)
                                    xs = X[:, bb * NT:(bb + 1) * NT, g * LG * DG:(g + 1) * LG * DG]
                                    link(nc.vector.tensor_tensor(xs, xs, Y[:, :, :, :].rearrange("p t h d -> p t (h d)"), ALU.add))
                stack.pop()
                end_phase(list(S.values()))

        with nc.Fori(0, B // NB, 1) as it:
            norm_phase(True, it)
            ffn_phase()
            norm_phase(False, it)
            mla_phase()
            norm_phase(False, it)
            ffn_phase()
            stored = sem("stored")
            with nc.Block() as block:
                @block.sync
                def _(sp):
                    for b in range(NB):
                        sp.dma_start(out[it * NB + b].rearrange("(t p) c -> p t c", p=P),
                                     X[:, b * NT:(b + 1) * NT, :]).then_inc(stored, 16)
                    sp.wait_ge(stored, 16 * NB)
            end_phase([stored])


_INS = ["L0_attn_x", "L0_attn_W_dq", "L0_attn_W_uq", "L0_attn_W_dkv", "L0_attn_W_uk", "L0_attn_W_uv", "L0_attn_W_o",
        "L0_ffn_wqkv", "L0_ffn_q_scale", "L0_ffn_k_scale", "L0_ffn_wo", "L0_ffn_ln_g", "L0_ffn_ln_b", "L0_ffn_w1",
        "L0_ffn_b1", "L0_ffn_w2", "L0_ffn_b2"]


def kernel(**inputs):
    import numpy as _np
    import concourse.bacc as _bacc
    from concourse import mybir as _mybir
    from concourse.bass_utils import run_bass_kernel_spmd as _run

    nc = _bacc.Bacc("TRN2", target_bir_lowering=False, num_devices=1)
    arrays, args = {}, []
    for name in _INS:
        a = _np.ascontiguousarray(inputs[name])
        arrays[f"in_{name}"] = a
        args.append(nc.dram_tensor(f"in_{name}", a.shape, _mybir.dt.from_np(a.dtype), kind="ExternalInput").ap())
    shape = tuple(inputs["L0_attn_x"].shape)
    c = shape_constants(shape[1])
    arrays["shape_constants"] = c
    args.append(nc.dram_tensor("shape_constants", c.shape, F32, kind="ExternalInput").ap())
    args.append(nc.dram_tensor("out_0", shape, F32, kind="ExternalOutput").ap())
    macaron(nc, *args)
    r = _run(nc, [arrays], core_ids=[0])
    return r.results[0]["out_0"]
```

```python
from contextlib import ExitStack

import numpy as np
import concourse.bass as bass
from concourse import mybir

F32 = mybir.dt.float32
F32R = mybir.dt.float32r
BF16 = mybir.dt.bfloat16
ALU = mybir.AluOpType
ACT = mybir.ActivationFunctionType
AX_X = mybir.AxisListType.X

P = 128
W = 64
NH, DH = 8, 64
NG, DG = 16, 8
EPS = 1e-5
BIG = -1e30
LG = 4


def shape_constants(T):
    half = np.arange(0, DH, 2, dtype=np.float32)
    inv = (1.0 / np.float32(10000.0) ** (half / np.float32(DH))).astype(np.float32)
    t = np.arange(T, dtype=np.float32)
    f = t[:, None] * inv[None, :]
    base = ((half + np.float32(0.4 * DH)) / np.float32(1.4 * DH)).astype(np.float32)
    power = ((t - T // 2) / np.float32(W // 2)).astype(np.float32)
    s = (base[None, :] ** power[:, None]).astype(np.float32)
    c, sn = np.cos(f), np.sin(f)
    tab = np.stack([np.concatenate([c * s, c * s], -1), np.concatenate([-sn * s, sn * s], -1),
                    np.concatenate([c / s, c / s], -1), np.concatenate([-sn / s, sn / s], -1)], 1)
    rope = tab.reshape(T // P, P, 4, DH).transpose(1, 0, 2, 3).reshape(P, -1).astype(np.float32)
    q, k = np.arange(P)[:, None] % W, np.arange(P)[None, :]
    band = np.where((k <= W + q) & (k >= q), 0.0, BIG).astype(np.float32)
    first = band.copy()
    first[:W, :W] = BIG
    causal = np.where(np.arange(P)[None, :] <= np.arange(P)[:, None], 0.0, BIG).astype(np.float32)
    row = np.arange(P)[:, None]
    headsel = row % (LG * DG) // DG == np.arange(LG)[None, :]
    low = [-1.0 * (row // (LG * DG) >= 2), -1.0 * (row // (LG * DG) % 2)]
    return np.concatenate([rope, band, first, causal, np.eye(P), headsel] + low, 1).astype(np.float32)


def macaron(nc, x, W_dq, W_uq, W_dkv, W_uk, W_uv, W_o, wqkv, q_scale, k_scale, wo, ln_g, ln_b,
            w1, b1, w2, b2, consts, out):
    B, T, C = x.shape
    DEPTH, HID = w2.shape[0], w2.shape[1]
    NT = T // P
    NB = 4
    NS = NB * NT
    QL = W_dq.shape[0]
    HC = -(-HID // 3)
    HCS = [HC, HC, HID - 2 * HC]
    CH = NH * DH // P
    GROUPS = NG // LG
    top = ExitStack()
    with top:
        stack = [top]
        phase = [0]

        def sb(name, shape, dt=F32):
            return stack[-1].enter_context(nc.sbuf_tensor(f"{name}_{phase[0]}", shape, dt))

        sems = {}

        def sem(name, kind="setup"):
            if (kind, name) not in sems:
                sems[kind, name] = top.enter_context(nc.semaphore(f"{name}_{kind}"))
            return sems[kind, name]

        BK = [top.enter_context(nc.psum_tensor(f"bank{i}", [P, 512], F32)) for i in range(8)]

        ROPE = NT * 4 * DH
        cst = sb("cst", [P, ROPE + 4 * P + LG + 2])
        ident = cst[:, ROPE + 3 * P:ROPE + 4 * P]
        headsel = cst[:, ROPE + 4 * P:ROPE + 4 * P + LG]
        low_rows = cst[:, ROPE + 4 * P + LG:ROPE + 4 * P + LG + 2]
        maskb = sb("maskb", [P, 3, P], BF16)
        identb = sb("identb", [P, P], BF16)
        ropet = sb("ropet", [P, DEPTH, NT, 4, DH])
        wqkv_h = sb("wqkv_h", [P, DEPTH, 3 * NH * DH])
        wqkv_l = sb("wqkv_l", [P, DEPTH, 3 * NH * DH])
        wo_s = sb("wo_s", [P, DEPTH, CH, P])
        w1_s = sb("w1_s", [P, DEPTH, 2 * HID])
        w2_s = sb("w2_s", [HC, DEPTH, 3, P])
        b1_s = sb("b1_s", [HC, DEPTH, 2, 3])
        b2_s = sb("b2_s", [P, DEPTH, P])
        lncol = sb("lncol", [P, 2 * DEPTH])
        meanw = sb("meanw", [P, P])
        ones = sb("ones", [P, P])
        mhalf = sb("mhalf", [P, 2 * NH])
        Wq_s = sb("Wq_s", [P, GROUPS, 4, LG * DG])
        Wk_s = sb("Wk_s", [P, GROUPS, 4, LG * DG])
        Wv_s = sb("Wv_s", [P, P])
        X = sb("X", [P, NS, P])
        U = sb("U", [P, NS, P])
        stats = sb("stats", [P, NS, 6])
        mv = sb("mv", [P, NS, 2])
        rstd = sb("rstd", [P, NS])

        def clear_all(used):
            engines = (nc.sync, nc.tensor, nc.scalar, nc.vector, nc.gpsimd)
            for n, s in enumerate(used):
                engines[n % len(engines)].sem_clear(s)
            nc.all_engine_barrier()

        with ExitStack() as scope:
            stack.append(scope)
            qs = sb("qs", [P, DEPTH, 2, DH])
            ks = sb("ks", [P, DEPTH, DH])
            dq = sb("dq", [QL, P]); uq = sb("uq", [P, QL]); dkv = sb("dkv", [QL, P])
            uk = sb("uk", [P, QL]); uv = sb("uv", [P, QL]); wom = sb("wom", [P, P])
            uqT = sb("uqT", [QL, P]); woT = sb("woT", [P, P]); WqT = sb("WqT", [P, P])
            keT = sb("keT", [QL, P]); ve = sb("ve", [QL, P])
            b1row = sb("b1row", [2 * DEPTH, HID]); lnrow = sb("lnrow", [2 * DEPTH, P])
            b1raw = sb("b1raw", [HC, 3, 2 * DEPTH])
            wqkv_raw = sb("wqkv_raw", [P, DEPTH, 3 * NH * DH])
            loaded = sem("loaded"); preset = sem("preset"); mm = sem("mm"); copied = sem("copied")
            columns = sem("columns"); high = sem("high")
            LOADS = [0]
            with nc.Block() as block:
                @block.sync
                def _(sp):
                    def load(dst, src):
                        sp.dma_start(dst, src).then_inc(loaded, 16)
                        LOADS[0] += 16
                    load(cst[:, :], consts)
                    load(dq[:, :], W_dq); load(uq[:, :], W_uq); load(dkv[:, :], W_dkv)
                    load(uk[:, :], W_uk); load(uv[:, :], W_uv); load(wom[:, :], W_o)
                    load(wqkv_raw[:, :, :], wqkv.rearrange("l p n -> p l n"))
                    load(w1_s[:, :, :], w1.rearrange("l p n -> p l n"))
                    for l in range(DEPTH):
                        load(wo_s[:, l, :, :], wo[l].rearrange("(c p) n -> p c n", p=P))
                    for c in range(3):
                        load(w2_s[0:HCS[c], :, c, :], w2[:, c * HC:c * HC + HCS[c], :].rearrange("l p n -> p l n"))
                    load(b1row[:, :], b1.rearrange("l (e h) -> (l e) h", e=2))
                    load(lnrow[0:DEPTH, :], ln_g)
                    load(lnrow[DEPTH:2 * DEPTH, :], ln_b)
                    load(b2_s[:, :, :].rearrange("p l n -> p (l n)"),
                         b2.rearrange("(a l) n -> a (l n)", a=1).broadcast_to([P, DEPTH * P]))
                    load(qs[:, :, 0, :], q_scale.unsqueeze(0).broadcast_to([P, DEPTH, DH]))
                    load(qs[:, :, 1, :], k_scale.unsqueeze(0).broadcast_to([P, DEPTH, DH]))
                NL = LOADS[0]

                @block.gpsimd
                def _(pool):
                    nc.gpsimd.memset(meanw[:, :], 1.0 / C).then_inc(preset, 1)
                    nc.gpsimd.memset(ones[:, :], 1.0).then_inc(preset, 1)
                    nc.gpsimd.memset(mhalf[:, :], -0.5).then_inc(preset, 1)
                    pool.wait_ge(high, 1)
                    nc.gpsimd.tensor_tensor(wqkv_l[:, :, :].bitcast(F32R), wqkv_raw[:, :, :], wqkv_h[:, :, :], ALU.subtract)

                @block.scalar
                def _(act):
                    act.wait_ge(loaded, NL)
                    nc.scalar.activation(wqkv_h[:, :, :].bitcast(F32R), wqkv_raw[:, :, :], ACT.Copy).then_inc(high, 1)

                @block.tensor
                def _(pe):
                    pe.wait_ge(loaded, NL)
                    pe.transpose(BK[0][0:QL, 0:P], uq[:, :], ident).then_inc(mm, 1)
                    pe.transpose(BK[1][:, 0:P], wom[:, :], ident).then_inc(mm, 1)
                    pe.transpose(BK[7][:, 0:2 * DEPTH], lnrow[:, :], ident[0:2 * DEPTH, 0:2 * DEPTH])
                    for c in range(3):
                        last = pe.transpose(BK[7][0:HCS[c], 8 * (c + 1):8 * (c + 1) + 2 * DEPTH],
                                            b1row[:, c * HC:c * HC + HCS[c]], ident[0:2 * DEPTH, 0:2 * DEPTH])
                    last.then_inc(mm, 1)
                    pe.wait_ge(copied, 1)
                    nc.tensor.matmul(BK[3][:, 0:P], uqT[:, :], dq[:, :], start=True, stop=True).then_inc(mm, 1)
                    nc.tensor.matmul(BK[4][:, 0:P], dq[:, :], uqT[:, :], start=True, stop=True).then_inc(mm, 1)
                    pe.wait_ge(copied, 2)
                    nc.tensor.matmul(BK[5][0:QL, 0:P], uv[:, :], woT[:, :], start=True, stop=True).then_inc(mm, 1)
                    pe.wait_ge(copied, 3)
                    nc.tensor.matmul(BK[6][0:QL, 0:P], uk[:, :], WqT[:, :], start=True, stop=True).then_inc(mm, 1)
                    pe.wait_ge(copied, 5)
                    nc.tensor.matmul(BK[0][:, 0:P], dkv[:, :], ve[:, :], start=True, stop=True).then_inc(mm, 1)
                    pe.wait_ge(copied, 6)
                    nc.tensor.matmul(BK[1][:, 0:P], dkv[:, :], keT[:, :], start=True, stop=True).then_inc(mm, 1)
                    pe.wait_ge(columns, 1)
                    for l in range(DEPTH):
                        for e in range(2):
                            for c in range(3):
                                o = e * HID + c * HC
                                j = (l * 2 + e) * 3 + c
                                last = nc.tensor.matmul(BK[2][0:HCS[c], j:j + 1], w1_s[:, l, o:o + HCS[c]],
                                                        lncol[:, DEPTH + l:DEPTH + l + 1], start=True, stop=True)
                    last.then_inc(mm, 1)

                @block.vector
                def _(dve):
                    dve.wait_ge(loaded, NL)
                    nc.vector.tensor_copy(maskb[:, :, :], cst[:, ROPE:ROPE + 3 * P].rearrange("p (a b) -> p a b", a=3))
                    nc.vector.tensor_copy(identb[:, :], ident)
                    dve.wait_ge(mm, 3)
                    nc.vector.tensor_copy(lncol[:, :], BK[7][:, 0:2 * DEPTH]).then_inc(columns, 1)
                    for c in range(3):
                        last = nc.vector.tensor_copy(b1raw[0:HCS[c], c, :], BK[7][0:HCS[c], 8 * (c + 1):8 * (c + 1) + 2 * DEPTH])
                    last.then_inc(columns, 1)

                    def stacked(bank):
                        return bank[:, 0:P].rearrange("p (g e) -> p g e", g=GROUPS).unsqueeze(2) \
                            .to_broadcast([P, GROUPS, 4, LG * DG])

                    for n, (dst, src, factor) in enumerate([
                            (uqT[:, :], BK[0][0:QL, 0:P], 1.0), (woT[:, :], BK[1][:, 0:P], 1.0),
                            (WqT[:, :], BK[3][:, 0:P], 1.0),
                            (Wq_s[:, :, :, :], stacked(BK[4]), float(DG) ** -0.5),
                            (ve[:, :], BK[5][0:QL, 0:P], 1.0), (keT[:, :], BK[6][0:QL, 0:P], 1.0),
                            (Wv_s[:, :], BK[0][:, 0:P], 1.0), (Wk_s[:, :, :, :], stacked(BK[1]), 1.0)]):
                        dve.wait_ge(mm, [1, 2, 4, 5, 6, 7, 8, 9][n])
                        nc.vector.tensor_scalar(dst, src, factor, None, ALU.mult).then_inc(copied, 1)
                    for l in range(DEPTH):
                        tab = cst[:, 0:ROPE].rearrange("p (t f d) -> p t f d", t=NT, f=4)
                        for f in range(4):
                            sc = qs[:, l, f // 2, :]
                            if f % 2:
                                for hf in range(2):
                                    other = sc[:, (1 - hf) * 32:(1 - hf) * 32 + 32]
                                    nc.vector.tensor_tensor(
                                        ropet[:, l, :, f, hf * 32:hf * 32 + 32], tab[:, :, f, hf * 32:hf * 32 + 32],
                                        other.unsqueeze(1).to_broadcast([P, NT, 32]), ALU.mult)
                            else:
                                nc.vector.tensor_tensor(ropet[:, l, :, f, :], tab[:, :, f, :],
                                                        sc.unsqueeze(1).to_broadcast([P, NT, DH]), ALU.mult)
                    dve.wait_ge(mm, 10)
                    dve.wait_ge(columns, 2)
                    for l in range(DEPTH):
                        for c in range(3):
                            j = l * 6 + c
                            nc.vector.tensor_tensor(b1_s[0:HCS[c], l, :, c], BK[2][0:HCS[c], j:j + 4:3],
                                                    b1raw[0:HCS[c], c, 2 * l:2 * l + 2], ALU.add)
                        nc.vector.tensor_scalar(w1_s[:, l, :], w1_s[:, l, :], lncol[:, l:l + 1], None, ALU.mult)
            stack.pop()
            clear_all([loaded, preset, mm, copied, columns, high])
            phase[0] += 1

        def norm_stats(dve, S, s):
            nc.vector.bn_stats(stats[:, s, :], X[:, s, :]).then_inc(S["st"], 1)
            dve.wait_ge(S["st"], 2 * s + 1)
            nc.vector.bn_aggr(mv[:, s, :], stats[:, s, :]).then_inc(S["st"], 1)
            if s % NT == NT - 1:
                dve.wait_ge(S["st"], 2 * s + 2)
                nc.vector.tensor_scalar(rstd[:, s - NT + 1:s + 1], mv[:, s - NT + 1:s + 1, 1], EPS, None,
                                        ALU.add).then_inc(S["nvar_ok"], 1)

        def norm_rstd(pool, S, b):
            sl = slice(b * NT, (b + 1) * NT)
            pool.wait_ge(S["nvar_ok"], b + 1)
            nc.gpsimd.tensor_tensor(rstd[:, sl], rstd[:, sl], mhalf[:, 0:NT], ALU.pow).then_inc(S["nrstd_ok"], 1)

        def norm_apply(dve, S, s):
            dve.wait_ge(S["nrstd_ok"], s // NT + 1)
            nc.vector.tensor_scalar(U[:, s, :], X[:, s, :], mv[:, s, 0:1], rstd[:, s:s + 1],
                                    ALU.subtract, ALU.mult).then_inc(S["u_ok"], 1)

        def ffn_phase(it, load, store, used):
            with ExitStack() as scope:
                stack.append(scope)
                HTH = sb("HTH", [P, 2, T + 1])
                HTL = sb("HTL", [P, 2, T + 1])
                HT2 = sb("HT2", [P, 2, T + 1])
                RA = sb("RA", [P, 2, 2, NH, DH])
                RB = sb("RB", [P, 2, NH, DH])
                SQ = sb("SQ", [P, 2 * NH, DH])
                SS = sb("SS", [P, 2 * NH])
                RN = sb("RN", [P, 2, 2 * NH])
                QZ = sb("QZ", [P, NH, P])
                KT = sb("KT", [P, CH, 2, W + T])
                VB = sb("VB", [P, 2, NT, NH, DH + 1])
                VA = sb("VA", [P, 2, NT, NH, DH + 1])
                PR = sb("PR", [P, NH, P])
                PT = sb("PT", [P, NH, P])
                NMX = sb("NMX", [P, NH])
                RS = sb("RS", [P, NH])
                ON = sb("ON", [P, NH, DH])
                OT = sb("OT", [P, CH, P])
                U2 = sb("U2", [P, 2, P])
                U2B = sb("U2B", [P, 2, P])
                DT = sb("DT", [P, P]); SQ2 = sb("SQ2", [P, P]); DG_ = sb("DG_", [P, P]); HN = sb("HN", [P, P])
                VE = sb("VE", [P, 1]); RV = sb("RV", [P, 1])
                GL = sb("GL", [HC, 3, P]); GLU = sb("GLU", [HC, 3, P])

                S = {n: sem(n, "ffn") for n in (
                    "preset uT_in u2T_in ht_ok ht2_ok q_in k_in v_in kmul qmul ksq sq_ok ss_ok qsum_ok ksum_ok rn_ok qrot_ok krot_ok hh_ok "
                    "qT_in kT_in qz_ok kt_ok s0_in s1_in nmx0_ok nmx1_ok p0_ok p1_ok pt0_in pt1_in pt0_ok pt1_ok vb_ok va_ok o_in on_ok "
                    "ot_in ot_ok wo_in u2_ok u2b_ok mean_in dt_ok sq2_ok var_in ve_ok rv_ok dg_ok bc_in hn_ok "
                    "w1a_in w1g_in gl_ok glu_ok w2_in u3_ok dch st nvar_ok nrstd_ok u_ok x_ok stored").split()}
                x_in = [sem(f"x_in{b}", "ffn") for b in range(NB)]
                NU = DEPTH * NS
                STEPS = range(NU + 7)
                B_UT, B_U2T, B_MEAN, B_VAR, B_BC = 6, 0, 5, 5, 3
                B_QKV, B_TURN = (3, 0, 5), (2, 7)
                B_S, B_PT, B_PV, B_OT, B_WO = (7, 1), (7, 1), (6, 1), 6, 3
                B_W1G, B_W1A, B_W2 = 2, 4, 4

                def unit(n):
                    s = n % NS
                    return n // NS, s // NT % 2, s % NT, s

                def live(n):
                    return 0 <= n < NU

                with nc.Block() as block:
                    @block.sync
                    def _(sp):
                        if load:
                            for b in range(NB):
                                sp.dma_start(X[:, b * NT:(b + 1) * NT, :],
                                             x[it * NB + b].rearrange("(t p) c -> p t c", p=P)).then_inc(x_in[b], 16)
                        for last_use in used:
                            sp.sem_clear(last_use)
                        if store:
                            for b in range(NB):
                                sp.wait_ge(S["x_ok"], NT * (b + 1))
                                sp.dma_start(out[it * NB + b].rearrange("(t p) c -> p t c", p=P),
                                             X[:, b * NT:(b + 1) * NT, :]).then_inc(S["stored"], 16)
                            sp.wait_ge(S["stored"], 16 * NB)

                    @block.tensor
                    def _(pe):
                        readers = [None] * 8

                        def claim(k, name, count):
                            if readers[k]:
                                pe.wait_ge(*readers[k])
                            readers[k] = (S[name], count)

                        def turn(u, g):
                            pe.wait_ge(S[("qrot_ok", "krot_ok")[g]], u + 1)
                            claim(B_TURN[g], ("qz_ok", "kt_ok")[g], u + 1)
                            for j in range(CH):
                                last = pe.transpose(BK[B_TURN[g]][:, j * P:(j + 1) * P],
                                                    RA[:, u % 2, g, 2 * j:2 * j + 2, :], ident)
                            last.then_inc(S[("qT_in", "kT_in")[g]], 1)

                        def project(u, k):
                            l, bb, t, s = unit(u)
                            tok, cols = slice(t * P, (t + 1) * P), slice(k * 512, (k + 1) * 512)
                            for n, (h, w) in enumerate(((HTH, wqkv_h), (HTH, wqkv_l), (HTL, wqkv_h))):
                                last = nc.tensor.matmul(BK[B_QKV[k]][:, :], h[:, bb, tok].bitcast(F32R),
                                                        w[:, l, cols].bitcast(F32R), start=(n == 0), stop=(n == 2))
                            return last

                        def scores(u, g):
                            l, bb, t, s = unit(u)
                            if u == 0:
                                pe.wait_ge(S["preset"], 5)
                            nc.tensor.matmul(BK[B_S[g]][:, :].rearrange("p (a b) -> p a b", a=4), identb[:, :],
                                             maskb[:, 1 if t == 0 else 0, :].unsqueeze(1).to_broadcast([P, 4, P]),
                                             start=True, stop=False, skip_group_check=True)
                            for h in range(4 * g, 4 * g + 4):
                                for w in range(2):
                                    k0 = (2 * t + w) * W
                                    last = nc.tensor.matmul(
                                        BK[B_S[g]][w * W:(w + 1) * W, (h % 4) * P:(h % 4 + 1) * P],
                                        QZ[:, h, w * W:(w + 1) * W], KT[:, h // 2, bb, k0:k0 + 2 * W],
                                        start=False, stop=True, skip_group_check=True)
                            return last

                        def hidden(l, g, k):
                            for j in range(3):
                                o = g * HID + j * HC
                                last = nc.tensor.matmul(BK[k][0:HCS[j], j * P:(j + 1) * P],
                                                        w1_s[:, l, o:o + HCS[j]], HN[:, :], start=True, stop=True)
                            return last

                        for n in STEPS:
                            u = n
                            if live(u):
                                if u >= NS:
                                    pe.wait_ge(S["u3_ok"], u - NS + 1)
                                else:
                                    pe.wait_ge(S["u_ok"], u + 1)
                                claim(B_UT, "ht_ok", u + 1)
                                pe.transpose(BK[B_UT][:, 0:P], U[:, unit(u)[3], :], ident).then_inc(S["uT_in"], 1)
                            u = n - 4
                            if live(u):
                                l = unit(u)[0]
                                pe.wait_ge(S["ot_ok"], u + 1)
                                claim(B_WO, "u2_ok", u + 1)
                                for j in range(CH):
                                    last = nc.tensor.matmul(BK[B_WO][:, 0:P], OT[:, j, :], wo_s[:, l, j, :],
                                                            start=(j == 0), stop=(j == CH - 1))
                                last.then_inc(S["wo_in"], 1)
                            u = n - 1
                            if live(u):
                                pe.wait_ge(S["ht_ok"], u + 1)
                                claim(B_QKV[2], "vb_ok", u + 1)
                                project(u, 2).then_inc(S["v_in"], 1)
                            u = n - 3
                            if live(u):
                                pe.wait_ge(S["p0_ok"], u + 1)
                                claim(B_PT[0], "pt0_ok", u + 1)
                                for h in range(4):
                                    last = pe.transpose(BK[B_PT[0]][:, h * P:(h + 1) * P], PR[:, 0 + h, :], ident)
                                last.then_inc(S["pt0_in"], 1)
                            u = n - 2
                            if live(u):
                                turn(u, 0)
                            u = n - 5
                            if live(u):
                                pe.wait_ge(S["dg_ok"], u + 1)
                                claim(B_BC, "hn_ok", u + 1)
                                nc.tensor.matmul(BK[B_BC][:, 0:P], ones[:, :], DG_[:, :],
                                                 start=True, stop=True).then_inc(S["bc_in"], 1)
                            u = n - 4
                            if live(u):
                                pe.wait_ge(S["u2_ok"], u + 1)
                                claim(B_U2T, "ht2_ok", u + 1)
                                pe.transpose(BK[B_U2T][:, 0:P], U2[:, u % 2, :], ident).then_inc(S["u2T_in"], 1)
                            u = n - 3
                            if live(u):
                                pe.wait_ge(S["p1_ok"], u + 1)
                                claim(B_PT[1], "pt1_ok", u + 1)
                                for h in range(4):
                                    last = pe.transpose(BK[B_PT[1]][:, h * P:(h + 1) * P], PR[:, 4 + h, :], ident)
                                last.then_inc(S["pt1_in"], 1)
                            u = n - 6
                            if live(u):
                                l = unit(u)[0]
                                pe.wait_ge(S["glu_ok"], u + 1)
                                claim(B_W2, "u3_ok", u + 1)
                                for j in range(3):
                                    last = nc.tensor.matmul(BK[B_W2][:, 0:P], GLU[0:HCS[j], j, :], w2_s[0:HCS[j], l, j, :],
                                                            start=(j == 0), stop=(j == 2))
                                last.then_inc(S["w2_in"], 1)
                            u = n - 2
                            if live(u):
                                turn(u, 1)
                            u = n
                            if live(u):
                                pe.wait_ge(S["ht_ok"], u + 1)
                                claim(B_QKV[0], "sq_ok", u + 1)
                                project(u, 0).then_inc(S["q_in"], 1)
                            u = n - 3
                            if live(u):
                                l, bb, t, s = unit(u)
                                pe.wait_ge(S["pt0_ok"], u + 1)
                                pe.wait_ge(S["pt1_ok"], u + 1)
                                pe.wait_ge(S["va_ok"], u + 1)
                                claim(B_PV[0], "on_ok", 2 * u + 1)
                                claim(B_PV[1], "on_ok", 2 * u + 2)
                                for h in range(NH):
                                    for w in range(2):
                                        o = (h % 4) * (DH + 1)
                                        last = nc.tensor.matmul(BK[B_PV[h // 4]][w * W:(w + 1) * W, o:o + DH + 1],
                                                                PT[:, h, w * W:(w + 1) * W], (VA, VB)[w][:, bb, t, h, :],
                                                                start=True, stop=True)
                                last.then_inc(S["o_in"], 1)
                            u = n
                            if live(u):
                                pe.wait_ge(S["ht_ok"], u + 1)
                                claim(B_QKV[1], "kmul", u + 1)
                                project(u, 1).then_inc(S["k_in"], 1)
                            u = n - 4
                            if live(u):
                                l, bb, t, s = unit(u)
                                pe.wait_ge(S["ht2_ok"], u + 1)
                                claim(B_MEAN, "dt_ok", u + 1)
                                nc.tensor.matmul(BK[B_MEAN][:, 0:P], meanw[:, :], HT2[:, bb, t * P:(t + 1) * P],
                                                 start=True, stop=True).then_inc(S["mean_in"], 1)
                            u = n - 5
                            if live(u):
                                pe.wait_ge(S["hn_ok"], u + 1)
                                claim(B_W1G, "gl_ok", u + 1)
                                hidden(unit(u)[0], 1, B_W1G).then_inc(S["w1g_in"], 1)
                            u = n - 2
                            if live(u):
                                pe.wait_ge(S["qz_ok"], u + 1)
                                pe.wait_ge(S["kt_ok"], u + 1)
                                claim(B_S[0], "p0_ok", u + 1)
                                scores(u, 0).then_inc(S["s0_in"], 1)
                            u = n - 3
                            if live(u):
                                pe.wait_ge(S["on_ok"], 2 * u + 2)
                                claim(B_OT, "ot_ok", u + 1)
                                for j in range(CH):
                                    last = pe.transpose(BK[B_OT][:, j * P:(j + 1) * P], ON[:, 2 * j:2 * j + 2, :], ident)
                                last.then_inc(S["ot_in"], 1)
                            u = n - 4
                            if live(u):
                                pe.wait_ge(S["sq2_ok"], u + 1)
                                claim(B_VAR, "ve_ok", u + 1)
                                nc.tensor.matmul(BK[B_VAR][:, 0:1], SQ2[:, :], meanw[:, 0:1],
                                                 start=True, stop=True).then_inc(S["var_in"], 1)
                            u = n - 2
                            if live(u):
                                claim(B_S[1], "p1_ok", u + 1)
                                scores(u, 1).then_inc(S["s1_in"], 1)
                            u = n - 5
                            if live(u):
                                pe.wait_ge(S["hn_ok"], u + 1)
                                claim(B_W1A, "glu_ok", u + 1)
                                hidden(unit(u)[0], 0, B_W1A).then_inc(S["w1a_in"], 1)

                    @block.scalar
                    def _(act):
                        def softmax_exp(u, g):
                            act.wait_ge(S[("nmx0_ok", "nmx1_ok")[g]], u + 1)
                            if u >= 1:
                                act.wait_ge(S[("pt0_in", "pt1_in")[g]], u)
                            for h in range(4):
                                last = nc.scalar.activation(PR[:, 4 * g + h, :], BK[B_S[g]][:, h * P:(h + 1) * P],
                                                            ACT.Exp, bias=NMX[:, 4 * g + h:4 * g + h + 1], scale=8.0)
                            return last

                        for n in STEPS:
                            u = n - 1
                            if live(u):
                                act.wait_ge(S["qmul"], u + 1)
                                if u >= 1:
                                    act.wait_ge(S["ss_ok"], u)
                                nc.scalar.activation(SQ[:, 0:NH, :], BK[B_QKV[0]][:, :].rearrange("p (h d) -> p h d", h=NH),
                                                     ACT.Square).then_inc(S["sq_ok"], 1)
                            u = n - 3
                            if live(u):
                                softmax_exp(u, 0).then_inc(S["p0_ok"], 1)
                            u = n - 3
                            if live(u):
                                softmax_exp(u, 1).then_inc(S["p1_ok"], 1)
                            u = n
                            if live(u):
                                l, bb, t, s = unit(u)
                                act.wait_ge(S["uT_in"], u + 1)
                                for lo, hi, c in ((0, W, t * P), (W, P, t * P + 1)):
                                    last = nc.scalar.activation(HTH[lo:hi, bb, c:c + P].bitcast(F32R), BK[B_UT][lo:hi, 0:P],
                                                                ACT.Copy)
                                last.then_inc(S["hh_ok"], 1)
                            u = n - 1
                            if live(u):
                                l, bb, t, s = unit(u)
                                act.wait_ge(S["v_in"], u + 1)
                                nc.scalar.activation(VB[:, bb, t, :, 0:DH], BK[B_QKV[2]][:, :].rearrange("p (h d) -> p h d", h=NH),
                                                     ACT.Copy).then_inc(S["vb_ok"], 1)
                            u = n - 3
                            if live(u):
                                act.wait_ge(S["pt1_in"], u + 1)
                                if u >= 1:
                                    act.wait_ge(S["o_in"], u)
                                nc.scalar.activation(PT[:, 4:8, :], BK[B_PT[1]][:, :].rearrange("p (h q) -> p h q", h=4),
                                                     ACT.Copy).then_inc(S["pt1_ok"], 1)
                            u = n - 2
                            if live(u):
                                act.wait_ge(S["qT_in"], u + 1)
                                if u >= 1:
                                    act.wait_ge(S["s1_in"], u)
                                for hf in range(2):
                                    src = BK[B_TURN[0]][hf * W:(hf + 1) * W, :].rearrange("p (c q) -> p c q", c=CH)
                                    last = nc.scalar.activation(QZ[hf * W:(hf + 1) * W, hf::2, :], src, ACT.Copy)
                                last.then_inc(S["qz_ok"], 1)
                            u = n - 5
                            if live(u):
                                l = unit(u)[0]
                                act.wait_ge(S["w1g_in"], u + 1)
                                if u >= 1:
                                    act.wait_ge(S["glu_ok"], u)
                                for j in range(3):
                                    last = nc.scalar.activation(GL[0:HCS[j], j, :], BK[B_W1G][0:HCS[j], j * P:(j + 1) * P],
                                                                ACT.Gelu, bias=b1_s[0:HCS[j], l, 1, j:j + 1])
                                last.then_inc(S["gl_ok"], 1)
                            u = n
                            if live(u):
                                act.wait_ge(S["k_in"], u + 1)
                                if u >= 1:
                                    act.wait_ge(S["ss_ok"], u)
                                nc.scalar.activation(SQ[:, NH:2 * NH, :], BK[B_QKV[1]][:, :].rearrange("p (h d) -> p h d", h=NH),
                                                     ACT.Square).then_inc(S["ksq"], 1)
                            u = n - 3
                            if live(u):
                                act.wait_ge(S["ot_in"], u + 1)
                                if u >= 1:
                                    act.wait_ge(S["wo_in"], u)
                                nc.scalar.activation(OT[:, :, :], BK[B_OT][:, :].rearrange("p (c q) -> p c q", c=CH),
                                                     ACT.Copy).then_inc(S["ot_ok"], 1)

                    @block.vector
                    def _(dve):
                        chain = [0]

                        def link(ins):
                            chain[0] += 1
                            ins.then_inc(S["dch"], 1)
                            dve.wait_ge(S["dch"], chain[0])

                        def rowmax(u, g):
                            dve.wait_ge(S[("s0_in", "s1_in")[g]], u + 1)
                            if u >= 1:
                                dve.wait_ge(S[("p0_ok", "p1_ok")[g]], u)
                            c = NMX[:, 4 * g:4 * g + 4]
                            link(nc.vector.tensor_reduce(c, BK[B_S[g]][:, :].rearrange("p (h q) -> p h q", h=4),
                                                         AX_X, ALU.max))
                            nc.vector.tensor_scalar(c, c, -8.0, None, ALU.mult).then_inc(S[("nmx0_ok", "nmx1_ok")[g]], 1)

                        def rotary(u, g):
                            l, bb, t, s = unit(u)
                            dve.wait_ge(S[("q_in", "k_in")[g]], u + 1)
                            if g == 1:
                                dve.wait_ge(S["ksq"], u + 1)
                            if u >= 1:
                                dve.wait_ge(S[("qsum_ok", "ksum_ok")[g]], u)
                            if u >= 2:
                                dve.wait_ge(S[("qT_in", "kT_in")[g]], u - 1)
                            bank = BK[B_QKV[g]]
                            src = bank[:, :].rearrange("p (h d) -> p h d", h=NH)
                            rot = bank[:, :].rearrange("p (h z d) -> p h z d", h=NH, z=2)[:, :, ::-1, :]
                            nc.vector.tensor_tensor(RA[:, u % 2, g, :, :], src,
                                                    ropet[:, l, t, 2 * g, :].unsqueeze(1).to_broadcast([P, NH, DH]),
                                                    ALU.mult)
                            tab = ropet[:, l, t, 2 * g + 1, :].rearrange("p (z d) -> p z d", z=2)
                            nc.vector.tensor_tensor(
                                RB[:, g, :, :].rearrange("p h (z d) -> p h z d", z=2), rot,
                                tab.unsqueeze(1).to_broadcast([P, NH, 2, DH // 2]),
                                ALU.mult).then_inc(S[("qmul", "kmul")[g]], 1)

                        def shifted(m, src, dst, inn, okk):
                            l, bb, t, s = unit(m)
                            dve.wait_ge(S[inn], m + 1)
                            nc.vector.tensor_copy(dst[0:W, bb, t * P:(t + 1) * P], BK[src][0:W, 0:P])
                            nc.vector.tensor_copy(dst[W:P, bb, t * P + 1:(t + 1) * P + 1],
                                                  BK[src][W:P, 0:P]).then_inc(S[okk], 1)

                        if load:
                            dve.wait_ge(x_in[0], 16)
                        for t in range(NT):
                            norm_stats(dve, S, t)
                        for t in range(NT):
                            norm_apply(dve, S, t)
                        for part in (HTH, HTL):
                            nc.vector.tensor_scalar(part[W:P, :, 0:1].bitcast(F32R), ones[W:P, 0:2].unsqueeze(2),
                                                    0.0, None, ALU.mult)
                        nc.vector.memset(HT2[W:P, :, 0:1], 0.0)
                        for n in STEPS:
                            u = n - 7
                            if live(u):
                                l = unit(u)[0]
                                dve.wait_ge(S["w1a_in"], u + 1)
                                dve.wait_ge(S["gl_ok"], u + 1)
                                if u >= 1:
                                    dve.wait_ge(S["w2_in"], u)
                                for j in range(3):
                                    h_ = HCS[j]
                                    last = nc.vector.scalar_tensor_tensor(
                                        out=GLU[0:h_, j, :], in0=BK[B_W1A][0:h_, j * P:(j + 1) * P],
                                        scalar=b1_s[0:h_, l, 0, j:j + 1], in1=GL[0:h_, j, :], op0=ALU.add, op1=ALU.mult)
                                last.then_inc(S["glu_ok"], 1)
                            u = n - 4
                            if live(u):
                                dve.wait_ge(S["pt0_in"], u + 1)
                                if u >= 1:
                                    dve.wait_ge(S["o_in"], u)
                                nc.vector.tensor_copy(PT[:, 0:4, :], BK[B_PT[0]][:, :].rearrange("p (h q) -> p h q", h=4)).then_inc(S["pt0_ok"], 1)
                            u = n - 6
                            if live(u):
                                dve.wait_ge(S["bc_in"], u + 1)
                                if u >= 1:
                                    dve.wait_ge(S["w1g_in"], u)
                                    dve.wait_ge(S["w1a_in"], u)
                                nc.vector.tensor_tensor(HN[:, :], BK[B_BC][:, 0:P], DT[:, :], ALU.mult).then_inc(S["hn_ok"], 1)
                            u = n - 1
                            if live(u):
                                l, bb, t, s = unit(u)
                                dve.wait_ge(S["hh_ok"], u + 1)
                                for lo, hi, c in ((0, W, t * P), (W, P, t * P + 1)):
                                    last = nc.vector.tensor_tensor(HTL[lo:hi, bb, c:c + P].bitcast(F32R), BK[B_UT][lo:hi, 0:P],
                                                                   HTH[lo:hi, bb, c:c + P], ALU.subtract)
                                last.then_inc(S["ht_ok"], 1)
                            u = n - 5
                            if live(u):
                                shifted(u, B_U2T, HT2, "u2T_in", "ht2_ok")
                            u = n - 2
                            if live(u):
                                dve.wait_ge(S["sq_ok"], u + 1)
                                dve.wait_ge(S["ksq"], u + 1)
                                if u >= 1:
                                    dve.wait_ge(S["rn_ok"], u)
                                link(nc.vector.tensor_reduce(SS[:, :], SQ[:, :, :], AX_X, ALU.add))
                                nc.vector.tensor_scalar(SS[:, :], SS[:, :], 1e-24, None, ALU.max).then_inc(S["ss_ok"], 1)
                            u = n - 7
                            if live(u):
                                l, bb, t, s = unit(u)
                                dve.wait_ge(S["w2_in"], u + 1)
                                dve.wait_ge(S["u2b_ok"], u + 1)
                                nc.vector.tensor_tensor(U[:, s, :], BK[B_W2][:, 0:P], U2B[:, u % 2, :],
                                                        ALU.add).then_inc(S["u3_ok"], 1)
                                if l == DEPTH - 1:
                                    dve.wait_ge(S["u3_ok"], u + 1)
                                    nc.vector.scalar_tensor_tensor(out=X[:, s, :], in0=U[:, s, :], scalar=0.5, in1=X[:, s, :],
                                                                   op0=ALU.mult, op1=ALU.add).then_inc(S["x_ok"], 1)
                            u = n
                            if NT <= u < NS:
                                norm_apply(dve, S, u)
                            u = n - 3
                            if live(u):
                                l, bb, t, s = unit(u)
                                dve.wait_ge(S["kT_in"], u + 1)
                                nc.vector.tensor_copy(KT[:, :, bb, W + t * P:W + (t + 1) * P],
                                                      BK[B_TURN[1]][:, :].rearrange("p (c q) -> p c q", c=CH)).then_inc(S["kt_ok"], 1)
                            u = n
                            if live(u) and u + NT < NS:
                                if load and u % NT == 0:
                                    dve.wait_ge(x_in[u // NT + 1], 16)
                                norm_stats(dve, S, u + NT)
                            u = n - 4
                            if live(u):
                                dve.wait_ge(S["o_in"], u + 1)
                                if u >= 1:
                                    dve.wait_ge(S["ot_in"], u)
                                for g in range(2):
                                    O = BK[B_PV[g]][:, 0:4 * (DH + 1)].rearrange("p (h d) -> p h d", h=4)
                                    link(nc.vector.reciprocal(RS[:, 4 * g:4 * g + 4], O[:, :, DH]))
                                    nc.vector.tensor_tensor(ON[:, 4 * g:4 * g + 4, :], O[:, :, 0:DH],
                                                            RS[:, 4 * g:4 * g + 4].unsqueeze(2).to_broadcast([P, 4, DH]),
                                                            ALU.mult).then_inc(S["on_ok"], 1)
                            u = n - 5
                            if live(u):
                                l, bb, t, s = unit(u)
                                dve.wait_ge(S["mean_in"], u + 1)
                                nc.vector.scalar_tensor_tensor(
                                    out=DT[:, :], in0=BK[B_MEAN][:, 0:P], scalar=-1.0, in1=HT2[:, bb, t * P:(t + 1) * P],
                                    op0=ALU.mult, op1=ALU.add).then_inc(S["dt_ok"], 1)
                                dve.wait_ge(S["dt_ok"], u + 1)
                                if u >= 1:
                                    dve.wait_ge(S["var_in"], u)
                                nc.vector.tensor_tensor(SQ2[:, :], DT[:, :], DT[:, :], ALU.mult).then_inc(S["sq2_ok"], 1)
                            u = n - 1
                            if live(u):
                                rotary(u, 0)
                            u = n - 3
                            if live(u):
                                rowmax(u, 0)
                            u = n - 3
                            if live(u):
                                l, bb, t, s = unit(u)
                                dve.wait_ge(S["vb_ok"], u + 1)
                                if u == 0:
                                    dve.wait_ge(S["preset"], 5)
                                if t < NT - 1:
                                    nc.vector.tensor_copy(VA[0:W, bb, t + 1, :, :], VB[W:P, bb, t, :, :])
                                nc.vector.tensor_copy(VA[W:P, bb, t, :, :], VB[0:W, bb, t, :, :]).then_inc(S["va_ok"], 1)
                            u = n - 5
                            if live(u):
                                dve.wait_ge(S["var_in"], u + 1)
                                if u >= 1:
                                    dve.wait_ge(S["rv_ok"], u)
                                nc.vector.tensor_scalar(VE[:, :], BK[B_VAR][:, 0:1], EPS, None, ALU.add).then_inc(S["ve_ok"], 1)
                            u = n - 3
                            if live(u):
                                rowmax(u, 1)
                            u = n - 1
                            if live(u):
                                rotary(u, 1)
                            u = n - 5
                            if live(u):
                                dve.wait_ge(S["rv_ok"], u + 1)
                                if u >= 1:
                                    dve.wait_ge(S["bc_in"], u)
                                nc.vector.tensor_scalar(DG_[:, :], ident, RV[:, 0:1], None, ALU.mult).then_inc(S["dg_ok"], 1)
                            u = n - 4
                            if live(u):
                                s = unit(u)[3]
                                dve.wait_ge(S["wo_in"], u + 1)
                                if u >= 2:
                                    dve.wait_ge(S["u2T_in"], u - 1)
                                    dve.wait_ge(S["u2b_ok"], u - 1)
                                nc.vector.tensor_tensor(U2[:, u % 2, :], BK[B_WO][:, 0:P], U[:, s, :], ALU.add).then_inc(S["u2_ok"], 1)

                    @block.gpsimd
                    def _(pool):
                        norm_rstd(pool, S, 0)
                        pool.wait_ge(S["nrstd_ok"], 1)
                        for k, (part, value) in enumerate((
                                (QZ[0:W, 1::2, :], 0.0), (QZ[W:P, 0::2, :], 0.0), (VB[:, :, :, :, DH:DH + 1], 1.0),
                                (KT[:, :, :, 0:W], 0.0), (VA[0:W, :, 0, :, :], 0.0))):
                            nc.gpsimd.memset(part, value).then_inc(S["preset"], 1)
                            pool.wait_ge(S["preset"], k + 1)
                        for n in STEPS:
                            u = n - 1
                            if live(u) and u + NT < NS and u % NT == NT - 1:
                                norm_rstd(pool, S, u // NT + 1)
                            u = n - 2
                            if live(u):
                                pool.wait_ge(S["qmul"], u + 1)
                                nc.gpsimd.tensor_tensor(RA[:, u % 2, 0, :, :], RA[:, u % 2, 0, :, :], RB[:, 0, :, :],
                                                        ALU.add).then_inc(S["qsum_ok"], 1)
                            u = n - 5
                            if live(u):
                                l = unit(u)[0]
                                pool.wait_ge(S["u2_ok"], u + 1)
                                if u >= 2:
                                    pool.wait_ge(S["u3_ok"], u - 1)
                                nc.gpsimd.tensor_tensor(U2B[:, u % 2, :], U2[:, u % 2, :], b2_s[:, l, :], ALU.add).then_inc(S["u2b_ok"], 1)
                            u = n - 2
                            if live(u):
                                pool.wait_ge(S["kmul"], u + 1)
                                nc.gpsimd.tensor_tensor(RA[:, u % 2, 1, :, :], RA[:, u % 2, 1, :, :], RB[:, 1, :, :],
                                                        ALU.add).then_inc(S["ksum_ok"], 1)
                            u = n - 2
                            if live(u):
                                pool.wait_ge(S["ss_ok"], u + 1)
                                nc.gpsimd.tensor_tensor(RN[:, u % 2, :], SS[:, :], mhalf[:, 0:2 * NH], ALU.pow).then_inc(S["rn_ok"], 1)
                            u = n - 5
                            if live(u):
                                pool.wait_ge(S["ve_ok"], u + 1)
                                if u >= 1:
                                    pool.wait_ge(S["dg_ok"], u)
                                nc.gpsimd.tensor_tensor(RV[:, :], VE[:, :], mhalf[:, 0:1], ALU.pow).then_inc(S["rv_ok"], 1)
                            u = n - 2
                            if live(u):
                                pool.wait_ge(S["rn_ok"], u + 1)
                                pool.wait_ge(S["qsum_ok"], u + 1)
                                nc.gpsimd.tensor_tensor(RA[:, u % 2, 0, :, :], RA[:, u % 2, 0, :, :],
                                                        RN[:, u % 2, 0:NH].unsqueeze(2).to_broadcast([P, NH, DH]),
                                                        ALU.mult).then_inc(S["qrot_ok"], 1)
                            u = n - 2
                            if live(u):
                                pool.wait_ge(S["rn_ok"], u + 1)
                                pool.wait_ge(S["ksum_ok"], u + 1)
                                nc.gpsimd.tensor_tensor(RA[:, u % 2, 1, :, :], RA[:, u % 2, 1, :, :],
                                                        RN[:, u % 2, NH:2 * NH].unsqueeze(2).to_broadcast([P, NH, DH]),
                                                        ALU.mult).then_inc(S["krot_ok"], 1)
                stack.pop()
                phase[0] += 1
                return list(S.values()) + x_in

        def mla_phase(used):
            with ExitStack() as scope:
                stack.append(scope)
                ALLG = NB * GROUPS
                UNITS = [(i, h0, n) for i, n in ((i, max(1, NT // (i + 1))) for i in range(NT))
                         for h0 in range(0, LG, n)]
                UN = len(UNITS)
                ON_DVE = [0, 0, 0, 0, 0, 0, 0, 0, 1, 0, 1]
                ALLU = ALLG * UN
                PT_LAG, PV_LAG, YT_LAG = 3, 5, 11
                EV_LAG, OT_LAG, Y_LAG = 3, 8, 11
                SRING, PRING = 4, 4
                B_PT, B_O, B_PREP = (4, 5), 6, 7
                XT_AT, Q_AT, K_AT = 1, 3, 5
                ROUND_Q, ROUND_K = 2, 4
                STEPS = ALLU + YT_LAG + 1

                def next_batch(m, g):
                    G = m // UN
                    b = G // GROUPS + 1
                    return b if b < NB and G % GROUPS == g and m % UN == XT_AT else None

                XT = sb("XT", [P, 2, T])
                RND = sb("RND", [P, 2, T])
                QS = sb("QS", [P, T])
                QZL = sb("QZL", [P, 2, LG, T])
                KL = sb("KL", [P, 2, T])
                VL = sb("VL", [P, 2, NT, NG, 32])
                PL = sb("PL", [P, PRING, T])
                PTL = sb("PTL", [P, 2, LG, NT, T])
                OTL = sb("OTL", [P, T])
                RL = sb("RL", [P, NT, LG])
                Y = sb("Y", [P, NT, LG, DG])
                NM = sb("NM", [P, SRING, LG])
                S = {n: sem(n, "mla") for n in (
                    "preset xt_in xt_ok q_in k_in v_in qr_ok kr_ok qs_ok kl_ok vl_ok qzd_ok qzp_ok s_in nm_ok p_ok pt_in "
                    "pta_ok ptd_ok o_in ot_ok y_in y_ok x_ok dch st nvar_ok nrstd_ok u_ok").split()}

                def evacuated(on_dve, m):
                    full, r = divmod(m + 1, UN)
                    n = sum(ON_DVE[:r]) + full * sum(ON_DVE)
                    return n if on_dve else m + 1 - n

                def group_end(m):
                    return m // UN if 0 <= m < ALLU and m % UN == UN - 1 else None

                def evac_args(m):
                    G, r = divmod(m, UN)
                    i, h0, n = UNITS[r]
                    return (PTL[:, G % 2, h0:h0 + n, 0:i + 1, i * P:(i + 1) * P],
                            BK[B_PT[m % 2]][:, 0:n * (i + 1) * P].rearrange("p (h j q) -> p h j q", h=n, q=P))

                with nc.Block() as block:
                    @block.sync
                    def _(sp):
                        for last_use in used:
                            sp.sem_clear(last_use)

                    @block.tensor
                    def _(pe):
                        readers = [None] * 8

                        def claim(k, name, count):
                            if readers[k]:
                                pe.wait_ge(*readers[k])
                            readers[k] = (S[name], count)

                        def xt(b):
                            pe.wait_ge(S["u_ok"], NT * (b + 1))
                            claim(B_PREP, "xt_ok", b + 1)
                            for t in range(NT):
                                last = pe.transpose(BK[B_PREP][:, t * P:(t + 1) * P], U[:, b * NT + t, :], ident)
                            last.then_inc(S["xt_in"], 1)

                        def values(b):
                            pe.wait_ge(S["xt_ok"], b + 1)
                            claim(B_PREP, "vl_ok", b + 1)
                            for t in range(NT):
                                last = nc.tensor.matmul(BK[B_PREP][:, t * P:(t + 1) * P], XT[:, b % 2, t * P:(t + 1) * P],
                                                        Wv_s[:, :], start=True, stop=True)
                            last.then_inc(S["v_in"], 1)

                        def queries(G):
                            b, g = divmod(G, GROUPS)
                            claim(B_PREP, "qs_ok", G + 1)
                            nc.tensor.matmul(BK[B_PREP][:, :], Wq_s[:, g, :, :], XT[:, b % 2, :],
                                             start=True, stop=True).then_inc(S["q_in"], 1)

                        def keys(G):
                            b, g = divmod(G, GROUPS)
                            claim(B_PREP, "kl_ok", G + 1)
                            nc.tensor.matmul(BK[B_PREP][:, :], Wk_s[:, g, :, :], XT[:, b % 2, :],
                                             start=True, stop=True).then_inc(S["k_in"], 1)

                        xt(0)
                        values(0)
                        queries(0)
                        keys(0)
                        for m in range(STEPS):
                            G, r = divmod(m, UN)
                            if next_batch(m, 1):
                                xt(next_batch(m, 1))
                            if next_batch(m, 2):
                                values(next_batch(m, 2))
                            if G + 1 < ALLG and r == Q_AT:
                                queries(G + 1)
                            if G + 1 < ALLG and r == K_AT:
                                keys(G + 1)
                            if m < ALLU:
                                i, h0, n = UNITS[r]
                                N = (i + 1) * P
                                if r == 0:
                                    pe.wait_ge(S["kl_ok"], G + 1)
                                    pe.wait_ge(S["qzd_ok"], G + 1)
                                    pe.wait_ge(S["qzp_ok"], G + 1)
                                claim(m % SRING, "p_ok", m + 1)
                                bank = BK[m % SRING]
                                for h in range(n):
                                    nc.tensor.matmul(bank[:, h * N:(h + 1) * N],
                                                     QZL[:, G % 2, h0 + h, i * P:(i + 1) * P].bitcast(F32R),
                                                     KL[:, G % 2, 0:N].bitcast(F32R),
                                                     start=(h == 0), stop=False, skip_group_check=True)
                                diag = bank[:, 0:n * N].rearrange("p (h k) -> p h k", h=n)[:, :, i * P:N]
                                nc.tensor.matmul(diag, identb[:, :], maskb[:, 2, :].unsqueeze(1).to_broadcast([P, n, P]),
                                                 start=False, stop=True, skip_group_check=True).then_inc(S["s_in"], 1)
                            k = m - PT_LAG
                            if 0 <= k < ALLU:
                                i, h0, n = UNITS[k % UN]
                                pe.wait_ge(S["p_ok"], k + 1)
                                on_dve = ON_DVE[k % UN]
                                claim(B_PT[k % 2], "ptd_ok" if on_dve else "pta_ok", evacuated(on_dve, k))
                                for j in range(n * (i + 1)):
                                    last = pe.transpose(BK[B_PT[k % 2]][:, j * P:(j + 1) * P],
                                                        PL[:, k % PRING, j * P:(j + 1) * P], ident)
                                last.then_inc(S["pt_in"], 1)
                            for j in range(NT):
                                g = group_end(m - PV_LAG - j)
                                if g is None:
                                    continue
                                if j == 0:
                                    pe.wait_ge(S["ptd_ok"], evacuated(True, m - PV_LAG))
                                    pe.wait_ge(S["pta_ok"], evacuated(False, m - PV_LAG))
                                    pe.wait_ge(S["vl_ok"], g // GROUPS + 1)
                                    if g == 0:
                                        pe.wait_ge(S["preset"], 1)
                                    claim(B_O, "ot_ok", g + 1)
                                for q in range(LG):
                                    last = nc.tensor.matmul(BK[B_O][32 * q:32 * q + 32, j * P:T],
                                                            VL[:, g // GROUPS % 2, j, g % GROUPS * LG + q, :],
                                                            PTL[:, g % 2, q, j, j * P:T],
                                                            start=(j == 0), stop=(j == NT - 1),
                                                            skip_group_check=True)
                                if j == NT - 1:
                                    last.then_inc(S["o_in"], 1)
                            g = group_end(m - YT_LAG)
                            if g is not None:
                                pe.wait_ge(S["ot_ok"], g + 1)
                                claim(B_PREP, "y_ok", g + 1)
                                for t in range(NT):
                                    last = pe.transpose(BK[B_PREP][:, t * P:(t + 1) * P], OTL[:, t * P:(t + 1) * P], ident)
                                last.then_inc(S["y_in"], 1)

                    @block.scalar
                    def _(act):
                        def values(b):
                            act.wait_ge(S["v_in"], b + 1)
                            nc.scalar.activation(VL[:, b % 2, :, :, 0:DG],
                                                 BK[B_PREP][:, :].rearrange("p (t h d) -> p t h d", t=NT, h=NG),
                                                 ACT.Copy).then_inc(S["vl_ok"], 1)

                        def high_q(G):
                            act.wait_ge(S["q_in"], G + 1)
                            if G >= 1:
                                act.wait_ge(S["qs_ok"], G)
                            nc.scalar.activation(RND[:, 0, :].bitcast(F32R), BK[B_PREP][:, :],
                                                 ACT.Copy).then_inc(S["qr_ok"], 1)

                        def high_k(G):
                            act.wait_ge(S["k_in"], G + 1)
                            if G >= 1:
                                act.wait_ge(S["kl_ok"], G)
                            nc.scalar.activation(RND[:, 1, :].bitcast(F32R), BK[B_PREP][:, :],
                                                 ACT.Copy).then_inc(S["kr_ok"], 1)

                        values(0)
                        high_q(0)
                        high_k(0)
                        for m in range(STEPS):
                            G, r = divmod(m, UN)
                            if next_batch(m, 2):
                                values(next_batch(m, 2))
                            if G + 1 < ALLG and r == ROUND_Q:
                                high_q(G + 1)
                            if G + 1 < ALLG and r == ROUND_K:
                                high_k(G + 1)
                            k = m - EV_LAG
                            if 0 <= k < ALLU and not ON_DVE[k % UN]:
                                act.wait_ge(S["pt_in"], k + 1)
                                if k // UN >= 2:
                                    act.wait_ge(S["o_in"], k // UN - 1)
                                dst, src = evac_args(k)
                                nc.scalar.activation(dst, src, ACT.Copy).then_inc(S["pta_ok"], 1)
                            if m < ALLU:
                                i, h0, n = UNITS[r]
                                N = (i + 1) * P
                                act.wait_ge(S["nm_ok"], m + 1)
                                if m >= PRING:
                                    act.wait_ge(S["pt_in"], m - PRING + 1)
                                for h in range(n):
                                    last = nc.scalar.activation(PL[:, m % PRING, h * N:(h + 1) * N],
                                                                BK[m % SRING][:, h * N:(h + 1) * N], ACT.Exp,
                                                                bias=NM[:, m % SRING, h:h + 1])
                                last.then_inc(S["p_ok"], 1)

                    @block.vector
                    def _(dve):
                        chain = [0]

                        def link(ins):
                            chain[0] += 1
                            ins.then_inc(S["dch"], 1)
                            dve.wait_ge(S["dch"], chain[0])

                        def xt(b):
                            dve.wait_ge(S["xt_in"], b + 1)
                            if b >= 2:
                                dve.wait_ge(S["k_in"], (b - 1) * GROUPS)
                                dve.wait_ge(S["q_in"], (b - 1) * GROUPS)
                            nc.vector.tensor_copy(XT[:, b % 2, :], BK[B_PREP][:, :]).then_inc(S["xt_ok"], 1)

                        def stack_q(G):
                            dve.wait_ge(S["qr_ok"], G + 1)
                            if G >= 1:
                                dve.wait_ge(S["qzp_ok"], G)
                            nc.vector.scalar_tensor_tensor(
                                out=QS[:, :].bitcast(F32R), in0=RND[:, 0, :], scalar=low_rows[:, 0:1],
                                in1=BK[B_PREP][:, :], op0=ALU.mult, op1=ALU.add).then_inc(S["qs_ok"], 1)

                        def pad_q(G):
                            dve.wait_ge(S["qs_ok"], G + 1)
                            if G >= 2:
                                dve.wait_ge(S["s_in"], (G - 1) * UN)
                            for h in range(2):
                                last = nc.vector.tensor_scalar(QZL[:, G % 2, h, :].bitcast(F32R), QS[:, :],
                                                               headsel[:, h:h + 1], None, ALU.mult)
                            last.then_inc(S["qzd_ok"], 1)

                        def stack_k(G):
                            dve.wait_ge(S["kr_ok"], G + 1)
                            if G >= 2:
                                dve.wait_ge(S["s_in"], (G - 1) * UN)
                            nc.vector.scalar_tensor_tensor(
                                out=KL[:, G % 2, :].bitcast(F32R), in0=RND[:, 1, :], scalar=low_rows[:, 1:2],
                                in1=BK[B_PREP][:, :], op0=ALU.mult, op1=ALU.add).then_inc(S["kl_ok"], 1)

                        for t in range(NT):
                            norm_stats(dve, S, t)
                        for t in range(NT):
                            norm_apply(dve, S, t)
                        xt(0)
                        stack_q(0)
                        stack_k(0)
                        pad_q(0)
                        for m in range(STEPS):
                            G, r = divmod(m, UN)
                            if m < ALLU and G % GROUPS == 0 and G // GROUPS + 1 < NB:
                                if r < NT:
                                    norm_stats(dve, S, (G // GROUPS + 1) * NT + r)
                                elif r >= UN - NT:
                                    norm_apply(dve, S, (G // GROUPS + 1) * NT + r - (UN - NT))
                            if next_batch(m, 1):
                                xt(next_batch(m, 1))
                            if G + 1 < ALLG and r == ROUND_Q + 1:
                                stack_q(G + 1)
                            if G + 1 < ALLG and r == ROUND_Q + 2:
                                pad_q(G + 1)
                            if G + 1 < ALLG and r == ROUND_K + 1:
                                stack_k(G + 1)
                            if m < ALLU:
                                i, h0, n = UNITS[r]
                                N = (i + 1) * P
                                dve.wait_ge(S["s_in"], m + 1)
                                if m >= SRING:
                                    dve.wait_ge(S["p_ok"], m - SRING + 1)
                                nc.vector.tensor_reduce(NM[:, m % SRING, 0:n],
                                                        BK[m % SRING][:, 0:n * N].rearrange("p (h k) -> p h k", h=n),
                                                        AX_X, ALU.max, negate=True).then_inc(S["nm_ok"], 1)
                            k = m - EV_LAG
                            if 0 <= k < ALLU and ON_DVE[k % UN]:
                                dve.wait_ge(S["pt_in"], k + 1)
                                if k // UN >= 2:
                                    dve.wait_ge(S["o_in"], k // UN - 1)
                                dst, src = evac_args(k)
                                nc.vector.tensor_copy(dst, src).then_inc(S["ptd_ok"], 1)
                            g = group_end(m - OT_LAG)
                            if g is not None:
                                dve.wait_ge(S["o_in"], g + 1)
                                if g >= 1:
                                    dve.wait_ge(S["y_in"], g)
                                nc.vector.tensor_copy(OTL[:, :], BK[B_O][:, :]).then_inc(S["ot_ok"], 1)
                            g = group_end(m - Y_LAG)
                            if g is not None:
                                dve.wait_ge(S["y_in"], g + 1)
                                O = BK[B_PREP][:, :].rearrange("p (t h d) -> p t h d", t=NT, h=LG)
                                link(nc.vector.reciprocal(RL[:, :, :], O[:, :, :, DG]))
                                if g >= 1:
                                    dve.wait_ge(S["x_ok"], g)
                                nc.vector.tensor_tensor(Y[:, :, :, :], O[:, :, :, 0:DG],
                                                        RL[:, :, :].unsqueeze(3).to_broadcast([P, NT, LG, DG]),
                                                        ALU.mult).then_inc(S["y_ok"], 1)

                    @block.gpsimd
                    def _(pool):
                        norm_rstd(pool, S, 0)
                        nc.gpsimd.memset(VL[:, :, :, :, DG:DG + 1], 1.0)
                        nc.gpsimd.memset(VL[:, :, :, :, DG + 1:32], 0.0).then_inc(S["preset"], 1)
                        for n in range(ALLG + 2):
                            if n % GROUPS == 1 and n // GROUPS + 1 < NB:
                                norm_rstd(pool, S, n // GROUPS + 1)
                            if n < ALLG:
                                pool.wait_ge(S["qs_ok"], n + 1)
                                if n >= 2:
                                    pool.wait_ge(S["s_in"], (n - 1) * UN)
                                for h in (2, 3):
                                    last = nc.gpsimd.tensor_scalar(QZL[:, n % 2, h, :].bitcast(F32R), QS[:, :],
                                                                   headsel[:, h:h + 1], None, ALU.mult)
                                last.then_inc(S["qzp_ok"], 1)
                            if n >= 2:
                                bb, g = divmod(n - 2, GROUPS)
                                pool.wait_ge(S["y_ok"], n - 1)
                                xs = X[:, bb * NT:(bb + 1) * NT, g * LG * DG:(g + 1) * LG * DG]
                                nc.gpsimd.tensor_tensor(xs, xs, Y[:, :, :, :].rearrange("p t h d -> p t (h d)"),
                                                        ALU.add).then_inc(S["x_ok"], 1)
                stack.pop()
                phase[0] += 1
                return list(S.values())

        with nc.Fori(0, B // NB, 1) as it:
            used = ffn_phase(it, load=True, store=False, used=[])
            used = mla_phase(used)
            clear_all(ffn_phase(it, load=False, store=True, used=used))


_INS = ["L0_attn_x", "L0_attn_W_dq", "L0_attn_W_uq", "L0_attn_W_dkv", "L0_attn_W_uk", "L0_attn_W_uv", "L0_attn_W_o",
        "L0_ffn_wqkv", "L0_ffn_q_scale", "L0_ffn_k_scale", "L0_ffn_wo", "L0_ffn_ln_g", "L0_ffn_ln_b", "L0_ffn_w1",
        "L0_ffn_b1", "L0_ffn_w2", "L0_ffn_b2"]


def kernel(**inputs):
    import numpy as _np
    import concourse.bacc as _bacc
    from concourse import mybir as _mybir
    from concourse.bass_utils import run_bass_kernel_spmd as _run

    nc = _bacc.Bacc("TRN2", target_bir_lowering=False, num_devices=1)
    arrays, args = {}, []
    for name in _INS:
        a = _np.ascontiguousarray(inputs[name])
        arrays[f"in_{name}"] = a
        args.append(nc.dram_tensor(f"in_{name}", a.shape, _mybir.dt.from_np(a.dtype), kind="ExternalInput").ap())
    shape = tuple(inputs["L0_attn_x"].shape)
    c = shape_constants(shape[1])
    arrays["shape_constants"] = c
    args.append(nc.dram_tensor("shape_constants", c.shape, F32, kind="ExternalInput").ap())
    args.append(nc.dram_tensor("out_0", shape, F32, kind="ExternalOutput").ap())
    macaron(nc, *args)
    r = _run(nc, [arrays], core_ids=[0])
    return r.results[0]["out_0"]
```
